# Optimizing a Trainium2 kernel written in Bass

```python
import numpy as np
import jax
import jax.numpy as jnp

def _softmax(x, axis=-1):
    return jax.nn.softmax(x, axis=axis)

def _gelu(x):
    return jax.nn.gelu(x, approximate=True)

def _silu(x):
    return jax.nn.silu(x)

def _sigmoid(x):
    return jax.nn.sigmoid(x)

def _layernorm(x, axis=-1, eps=1e-05):
    m = jnp.mean(x, axis=axis, keepdims=True)
    v = jnp.var(x, axis=axis, keepdims=True)
    return (x - m) / jnp.sqrt(v + eps)

def _scatter_add(tgt, idx, src, axis=0):
    return tgt.at[idx].add(src)

def _segment_sum(src, seg, n):
    return jax.ops.segment_sum(src, seg, n)
kernel_name = 'mk_hybrid_d1_jaxref_r4_cbfbf7'

def setup_inputs(seed: int=0):
    np.random.seed(seed)
    _w = jnp.asarray

    def _L0_attn_a_setup():
        import jax, jax.numpy as jnp
        import numpy as np
        D_MODEL = 256
        N_HEAD = 16
        SEQ = 512
        BATCH = 2
        key = jax.random.key(seed)
        x = jax.random.normal(key, (BATCH, SEQ, D_MODEL), dtype=jnp.float32)
        return {'x': x}
    _L0_attn_a_in = _L0_attn_a_setup()

    def _L0_attn_b_setup():
        import jax, jax.numpy as jnp
        import numpy as np
        B, S, D = (4, 512, 256)
        GAMMA = 1.0
        key = jax.random.key(seed)
        ks = jax.random.split(key, 9)
        scale = 1.0 / np.sqrt(D)
        return {'x': jax.random.normal(ks[0], (B, S, D), dtype=jnp.float32), 'Wq': jax.random.normal(ks[1], (D, D), dtype=jnp.float32) * scale, 'bq': jax.random.normal(ks[2], (D,), dtype=jnp.float32) * 0.01, 'Wk': jax.random.normal(ks[3], (D, D), dtype=jnp.float32) * scale, 'bk': jax.random.normal(ks[4], (D,), dtype=jnp.float32) * 0.01, 'Wv': jax.random.normal(ks[5], (D, D), dtype=jnp.float32) * scale, 'bv': jax.random.normal(ks[6], (D,), dtype=jnp.float32) * 0.01, 'Wo': jax.random.normal(ks[7], (D, D), dtype=jnp.float32) * scale, 'bo': jax.random.normal(ks[8], (D,), dtype=jnp.float32) * 0.01}
    _L0_attn_b_in = _L0_attn_b_setup()

    def _L0_ffn_setup():
        import jax, jax.numpy as jnp
        import numpy as np
        B, T, D, F_FF, E, K = (8, 512, 256, 1024, 8, 2)
        key = jax.random.key(seed)
        ks = jax.random.split(key, 6)
        s = 1.0 / np.sqrt(D)
        return {'x': jax.random.normal(ks[0], (B, T, D), jnp.float32), 'Wr': jax.random.normal(ks[1], (D, E), jnp.float32) * s, 'W1': jax.random.normal(ks[2], (E, D, F_FF), jnp.float32) * s, 'b1': jax.random.normal(ks[3], (E, F_FF), jnp.float32) * 0.01, 'W2': jax.random.normal(ks[4], (E, F_FF, D), jnp.float32) * (1.0 / np.sqrt(F_FF)), 'b2': jax.random.normal(ks[5], (E, D), jnp.float32) * 0.01}
    _L0_ffn_in = _L0_ffn_setup()
    _d = {'L0_attn_a_x': _L0_attn_a_in['x'], 'L0_attn_b_Wq': _L0_attn_b_in['Wq'], 'L0_attn_b_bq': _L0_attn_b_in['bq'], 'L0_attn_b_Wk': _L0_attn_b_in['Wk'], 'L0_attn_b_bk': _L0_attn_b_in['bk'], 'L0_attn_b_Wv': _L0_attn_b_in['Wv'], 'L0_attn_b_bv': _L0_attn_b_in['bv'], 'L0_attn_b_Wo': _L0_attn_b_in['Wo'], 'L0_attn_b_bo': _L0_attn_b_in['bo'], 'L0_ffn_Wr': _L0_ffn_in['Wr'], 'L0_ffn_W1': _L0_ffn_in['W1'], 'L0_ffn_b1': _L0_ffn_in['b1'], 'L0_ffn_W2': _L0_ffn_in['W2'], 'L0_ffn_b2': _L0_ffn_in['b2']}
    _x0 = _d['L0_attn_a_x']
    _d['L0_attn_a_x'] = jax.random.normal(jax.random.fold_in(jax.random.key(seed), 1), (2, 2048, 256), dtype=_x0.dtype)
    del _x0
    return _d

def reference(L0_attn_a_x, L0_attn_b_Wq, L0_attn_b_bq, L0_attn_b_Wk, L0_attn_b_bk, L0_attn_b_Wv, L0_attn_b_bv, L0_attn_b_Wo, L0_attn_b_bo, L0_ffn_Wr, L0_ffn_W1, L0_ffn_b1, L0_ffn_W2, L0_ffn_b2):

    def _L0_attn_a_ref(x):
        import jax, jax.numpy as jnp
        import numpy as np
        D_MODEL = 256
        N_HEAD = 16
        SEQ = 512
        BATCH = 2
        B, S, D = x.shape
        H = N_HEAD
        hd = D // H
        qkv = x.reshape(B, S, H, hd).transpose(0, 2, 1, 3)
        q = k = v = qkv
        w = jnp.einsum('bhqd,bhkd->bhqk', q, k) / jnp.sqrt(jnp.asarray(hd, x.dtype))
        causal = jnp.tril(jnp.ones((S, S), dtype=bool))
        mask_value = jnp.finfo(w.dtype).min
        w = jnp.where(causal[None, None, :, :], w, mask_value)
        w = jax.nn.softmax(w, axis=-1)
        out = jnp.einsum('bhqk,bhkd->bhqd', w, v)
        return out.transpose(0, 2, 1, 3).reshape(B, S, D)

    def _L0_attn_b_ref(x, Wq, bq, Wk, bk, Wv, bv, Wo, bo):
        import jax, jax.numpy as jnp
        import numpy as np
        B, S, D = (4, 512, 256)
        GAMMA = 1.0
        q = x @ Wq + bq
        k = x @ Wk + bk
        v = x @ Wv + bv
        q_sq = jnp.sum(q * q, axis=-1)
        k_sq = jnp.sum(k * k, axis=-1)
        qk = jnp.einsum('bqd,bkd->bqk', q, k)
        dist_sq = q_sq[:, :, None] + k_sq[:, None, :] - 2.0 * qk
        scores = jnp.exp(-GAMMA * dist_sq)
        attn = jax.nn.softmax(scores, axis=-1)
        out = jnp.einsum('bqk,bkd->bqd', attn, v)
        return out @ Wo + bo

    def _L0_ffn_ref(x, Wr, W1, b1, W2, b2):
        import jax, jax.numpy as jnp
        import numpy as np
        B, T, D, F_FF, E, K = (8, 512, 256, 1024, 8, 2)
        pooled = x.mean(axis=1)
        logits = pooled @ Wr
        top_scores, top_idx = jax.lax.top_k(logits, K)
        weights = jax.nn.softmax(top_scores, axis=-1)
        W1s, b1s = (W1[top_idx], b1[top_idx])
        W2s, b2s = (W2[top_idx], b2[top_idx])
        h = jnp.einsum('btd,bkdf->bktf', x, W1s) + b1s[:, :, None, :]
        h = jax.nn.gelu(h, approximate=False)
        y = jnp.einsum('bktf,bkfd->bktd', h, W2s) + b2s[:, :, None, :]
        out = jnp.einsum('bk,bktd->btd', weights, y)
        return out
    x = L0_attn_a_x
    x = x + _L0_attn_a_ref(_layernorm(x, axis=-1))
    x = x + _L0_ffn_ref(_layernorm(x, axis=-1), L0_ffn_Wr, L0_ffn_W1, L0_ffn_b1, L0_ffn_W2, L0_ffn_b2)
    x = x + _L0_attn_b_ref(_layernorm(x, axis=-1), L0_attn_b_Wq, L0_attn_b_bq, L0_attn_b_Wk, L0_attn_b_bk, L0_attn_b_Wv, L0_attn_b_bv, L0_attn_b_Wo, L0_attn_b_bo)
    x = x + _L0_ffn_ref(_layernorm(x, axis=-1), L0_ffn_Wr, L0_ffn_W1, L0_ffn_b1, L0_ffn_W2, L0_ffn_b2)
    return x

_drawn_inputs = setup_inputs


def setup_inputs(seed=0):
    import zlib

    import numpy as np

    out = dict(_drawn_inputs(seed))
    spreads = {}
    factors = {'L0_attn_b_bv': 7.633, 'L0_attn_b_bo': 8.0, 'L0_ffn_b1': 8.0, 'L0_ffn_b2': 6.736}
    for name, (base, spread) in spreads.items():
        noise = np.random.default_rng([zlib.crc32(name.encode()), seed]).standard_normal(out[name].shape)
        drawn = base * np.exp(spread * noise) if base else spread * noise
        out[name] = jnp.asarray(drawn.astype(out[name].dtype))
    for name, factor in factors.items():
        out[name] = (out[name] * factor).astype(out[name].dtype)
    return out
```

```python
from contextlib import ExitStack

import numpy as np

import concourse.bass as bass
from concourse import mybir

F32 = mybir.dt.float32
F32R = mybir.dt.float32r
F16 = mybir.dt.float16
U32 = mybir.dt.uint32
ALU = mybir.AluOpType
ACT = mybir.ActivationFunctionType
AX = mybir.AxisListType

P = 128
EPS = 1e-5
NB, S, D = 2, 2048, 256
TILES = S // P
CHUNK = 512
CHUNKS = S // CHUNK
TPC = CHUNK // P
KD = D // P
HEADS, HD = 16, 16
PAIRS = HEADS // 2
GROUPS = HEADS // 4
E, F = 8, 1024
FT = F // P
TOPK = 2


class Program:

    def __init__(self, nc, ctx, args):
        self.nc, self.stage_sems = nc, []
        self.s_out = nc.alloc_semaphore(name="out_stored")
        (self.x_d, self.Wq, self.bq, self.Wk, self.bk, self.Wv, self.bv, self.Wo, self.bo,
         self.Wr, self.W1, self.b1, self.W2, self.b2, self.out_d) = args
        sb = self.sb(ctx)
        self.x = sb("x", [P, NB * TILES, D], F32)
        self.ident = sb("ident", [P, P], F32)
        self.ident16 = sb("ident16", [P, P], F16)
        self.ones = sb("ones", [P, P], F32)
        self.wr = sb("wr", [P, KD, E], F32)
        self.stats = sb("stats", [P, TILES, 6], F32)
        self.mv = sb("mv", [P, TILES, 2], F32)
        self.vare = sb("vare", [P, TILES], F32)
        self.std = sb("std", [P, TILES], F32)
        self.nrm = sb("nrm", [P, 4, TILES], F32)
        self.rstd = self.nrm[:, 3, :]
        self.bias_b = sb("bias_b", [P, 4, KD], F32)
        self.bvo = sb("bvo", [P, KD], F32)

    def sb(self, ctx):
        return lambda name, shape, dt: ctx.enter_context(self.nc.sbuf_tensor(name, shape, dt))

    def ps(self, ctx):
        return lambda name, shape, dt: ctx.enter_context(self.nc.psum_tensor(name, shape, dt))

    def sems(self, stage, *names):
        made = [self.nc.alloc_semaphore(name=f"{stage}_{n}") for n in names]
        self.stage_sems += made
        return made

    def end_stage(self):
        self.nc.clear_and_free_semaphores(self.stage_sems)
        self.nc.all_engine_barrier()
        self.stage_sems = []

    def norm_sems(self, stage):
        return self.sems(stage, "stats", "aggr", "vare", "sqrt", "newton")

    def norm_vector(self, dve, b, sems):
        s_stats, s_aggr, s_vare, s_sqrt, s_newton = sems
        for t in range(TILES):
            dve.bn_stats(self.stats[:, t, :], self.x[:, b * TILES + t, :]).then_inc(s_stats, 1)
        for t in range(TILES):
            dve.wait_ge(s_stats, t + 1)
            dve.bn_aggr(self.mv[:, t, :], self.stats[:, t, :]).then_inc(s_aggr, 1)
        dve.wait_ge(s_aggr, TILES)
        dve.tensor_scalar(self.vare[:], self.mv[:, :, 1], EPS, None, ALU.add).then_inc(s_vare, 1)
        dve.wait_ge(s_sqrt, 1)
        dve.reciprocal(self.nrm[:, 0, :], self.std[:]).then_inc(s_newton, 1)
        dve.wait_ge(s_newton, 1)
        dve.tensor_tensor(self.nrm[:, 1, :], self.vare[:], self.nrm[:, 0, :], ALU.mult).then_inc(s_newton, 1)
        dve.wait_ge(s_newton, 2)
        dve.tensor_tensor(self.nrm[:, 2, :], self.nrm[:, 1, :], self.std[:], ALU.add).then_inc(s_newton, 1)
        dve.wait_ge(s_newton, 3)
        dve.reciprocal(self.nrm[:, 0, :], self.nrm[:, 2, :]).then_inc(s_newton, 1)
        dve.wait_ge(s_newton, 4)
        dve.tensor_scalar(self.rstd, self.nrm[:, 0, :], 2.0, None, ALU.mult).then_inc(s_newton, 1)
        dve.wait_ge(s_newton, 5)

    def norm_scalar(self, act, sems):
        act.wait_ge(sems[2], 1)
        act.activation(self.std[:], self.vare[:], ACT.Sqrt).then_inc(sems[3], 1)


def setup(pr):
    nc = pr.nc
    s_x, s_w, s_zero, s_made, s_turned = pr.sems("setup", "x", "w", "zero", "made", "turned")
    with ExitStack() as ctx:
        bias_rows = pr.sb(ctx)("bias_rows", [4 * KD, P], F32)
        bias_cols = pr.ps(ctx)("bias_cols", [P, 4 * KD], F32)
        block = ctx.enter_context(nc.Block())

        @block.tensor
        def _(pe):
            pe.wait_ge(s_w, 5 * 16)
            pe.wait_ge(s_made, 3)
            pe.transpose(bias_cols[:], bias_rows[:], pr.ident[0:4 * KD, 0:4 * KD]).then_inc(s_turned, 1)

        @block.vector
        def _(dve):
            dve.wait_ge(s_turned, 1)
            dve.tensor_copy(pr.bias_b[:].rearrange("p i k -> p (i k)"), bias_cols[:])

        @block.sync
        def _(sp):
            for i in range(8):
                n = NB * TILES // 8
                sp.dma_start(pr.x[:, n * i:n * i + n, :], pr.x_d.rearrange("b (t p) d -> p (b t) d", p=P)[:, n * i:n * i + n, :])\
                    .then_inc(s_x, 16)
            sp.wait_ge(s_x, 8 * 16)
            sp.wait_ge(s_w, 5 * 16)

        @block.scalar
        def _(act):
            act.dma_start(pr.wr[:], pr.Wr.rearrange("(k p) e -> p k e", p=P)).then_inc(s_w, 16)
            for i, v in enumerate((pr.bq, pr.bk, pr.bv, pr.bo)):
                act.dma_start(bias_rows[KD * i:KD * i + KD, :], v.rearrange("(k p) -> k p", p=P)).then_inc(s_w, 16)

        @block.gpsimd
        def _(pool):
            pool.memset(pr.ident[:], 0.0).then_inc(s_zero, 1)
            pool.memset(pr.ident16[:], 0.0).then_inc(s_zero, 1)
            pool.memset(pr.ones[:], 1.0).then_inc(s_made, 1)
            pool.wait_ge(s_zero, 2)
            for m in (pr.ident, pr.ident16):
                pool.affine_select(out=m[:], in_=m[:], compare_op=ALU.not_equal, fill=1.0, base=0,
                                   pattern=[[-1, P]], channel_multiplier=1).then_inc(s_made, 1)


def head_attention(pr, b):
    nc, x = pr.nc, pr.x
    st = f"a{b}"
    with ExitStack() as ctx:
        sb, ps = pr.sb(ctx), pr.ps(ctx)
        values = sb(f"{st}_values", [P, TILES, HEADS, 32], F32)
        moving = sb(f"{st}_moving", [P, PAIRS, S], F16)
        fixed = sb(f"{st}_fixed", [P, HEADS, S], F16)
        ZR = 3
        split_m = sb(f"{st}_split_m", [P, ZR, HEADS, 2, 2, HD], F16)
        split_f = sb(f"{st}_split_f", [P, ZR, HEADS, 2, 2, HD], F16)
        UR = 4
        probs = sb(f"{st}_probs", [P, UR, 2, CHUNK], F32)
        osb = sb(f"{st}_osb", [P, 2, CHUNK], F32)
        rden = sb(f"{st}_rden", [P, TPC, 4], F32)
        onorm = sb(f"{st}_onorm", [P, TPC, 4, HD], F32)
        SR = 3
        scores = ps(f"{st}_scores", [P, 2 * SR, CHUNK], F32)
        turned = scores[:].bitcast(F16)
        heads_out = ps(f"{st}_out", [P, 2, CHUNK], F32)

        nsems = pr.norm_sems(st)
        (s_zero, s_xn, s_hi, s_lo_m, s_lo_f, s_tmov, s_tfix, s_emov, s_efix, s_scores, s_exp, s_mask, s_pv, s_ocopy,
         s_oturn, s_rden, s_onorm, s_added) = pr.sems(
            st, "zero", "xn", "hi", "lo_m", "lo_f", "tmov", "tfix", "emov", "efix", "scores", "exp", "mask", "pv",
            "ocopy", "oturn", "rden", "onorm", "added")

        steps, group_end = [], []
        for c in range(CHUNKS):
            for g in range(GROUPS):
                for kt in range(TPC * (c + 1)):
                    steps.append((c, g, kt))
                group_end.append(len(steps))
        masked = []
        for n, (c, g, kt) in enumerate(steps):
            if kt >= TPC * c:
                masked += [2 * n, 2 * n + 1]
        masks_by = [sum(1 for u in masked if u <= i) for i in range(2 * len(steps))]

        def span(c, kt):
            skip = max(0, kt - TPC * c) * P
            return skip, CHUNK - skip

        with nc.Block() as block:
            @block.vector
            def _(dve):
                dve.memset(fixed[:].bitcast(F32), 0.0).then_inc(s_zero, 1)
                pr.norm_vector(dve, b, nsems)
                for t in range(TILES + 2):
                    if t < TILES:
                        dve.tensor_scalar(values[:, t, :, 0:HD], x[:, b * TILES + t, :].rearrange("p (h e) -> p h e", h=HEADS),
                                          pr.mv[:, t, 0:1], pr.rstd[:, t:t + 1], ALU.subtract, ALU.mult).then_inc(s_xn, 1)
                    if 1 <= t <= TILES:
                        u = t - 1
                        dve.wait_ge(s_hi, 2 * u + 2)
                        twice = values[:, u, :, 0:HD].unsqueeze(2).to_broadcast([P, HEADS, 2, HD])
                        dve.tensor_tensor(split_m[:, u % ZR, :, :, 1, :], twice, split_m[:, u % ZR, :, :, 0, :],
                                          ALU.subtract).then_inc(s_lo_m, 1)
                    if t >= 2:
                        u = t - 2
                        dve.wait_ge(s_tfix, u + 1)
                        if u == 0:
                            dve.wait_ge(s_zero, 1)
                        view = fixed[:, :, u * P:(u + 1) * P].rearrange("p (r a) n -> p r a n", a=2)
                        src = turned[:, 3 + u % 3, :].rearrange("p (r n) -> p r n", r=PAIRS)
                        dve.tensor_copy(view[0:64, :, 0, :], src[0:64]).then_inc(s_efix, 1)
                        dve.tensor_copy(view[64:128, :, 1, :], src[64:128]).then_inc(s_efix, 1)
                for i, (c, g) in enumerate((c, g) for c in range(CHUNKS) for g in range(GROUPS)):
                    bank = i % 2
                    dve.wait_ge(s_pv, group_end[i])
                    dve.tensor_copy(osb[:, bank, :], heads_out[:, bank, :]).then_inc(s_ocopy, 1)
                    dve.wait_ge(s_oturn, i + 1)
                    o = heads_out[:, bank, :].rearrange("p (t j e) -> p t j e", t=TPC, j=4)
                    dve.reciprocal(rden[:], o[:, :, :, HD]).then_inc(s_rden, 1)
                    dve.wait_ge(s_rden, i + 1)
                    dve.tensor_tensor(onorm[:], o[:, :, :, 0:HD], rden[:].unsqueeze(3).to_broadcast([P, TPC, 4, HD]),
                                      ALU.mult).then_inc(s_onorm, 1)
                    dve.wait_ge(s_onorm, i + 1)
                    xv = x[:, b * TILES + c * TPC:b * TILES + (c + 1) * TPC, 64 * g:64 * g + 64]\
                        .rearrange("p t (j e) -> p t j e", j=4)
                    dve.tensor_tensor(xv, xv, onorm[:], ALU.add).then_inc(s_added, 1)

            @block.scalar
            def _(act):
                pr.norm_scalar(act, nsems)
                for t in range(TILES + 2):
                    if t < TILES:
                        act.wait_ge(s_xn, t + 1)
                        if t >= ZR:
                            act.wait_ge(s_tmov, t - ZR + 1)
                            act.wait_ge(s_tfix, t - ZR + 1)
                        twice = values[:, t, :, 0:HD].unsqueeze(2).to_broadcast([P, HEADS, 2, HD])
                        act.activation(split_m[:, t % ZR, :, :, 0, :], twice, ACT.Copy).then_inc(s_hi, 1)
                        act.activation(split_f[:, t % ZR, :, 0, :, :], twice, ACT.Copy).then_inc(s_hi, 1)
                    if t >= 2:
                        u = t - 2
                        act.wait_ge(s_tmov, u + 1)
                        act.activation(moving[:, :, u * P:(u + 1) * P],
                                       turned[:, u % 3, :].rearrange("p (r n) -> p r n", r=PAIRS), ACT.Copy).then_inc(s_emov, 1)
                for n, (c, g, kt) in enumerate(steps):
                    skip, w = span(c, kt)
                    for a in range(2):
                        u = 2 * n + a
                        act.wait_ge(s_scores, u + 1)
                        if u >= UR:
                            act.wait_ge(s_pv, (u - UR) // 2 + 1)
                        act.activation(probs[:, u % UR, :, 0:w], scores[:, 2 * (u % SR):2 * (u % SR) + 2, 0:w], ACT.Exp,
                                       scale=HD ** -0.5).then_inc(s_exp, 1)

            @block.gpsimd
            def _(pool):
                pool.memset(values[:, :, :, HD:32], 1.0).then_inc(s_zero, 1)
                for t in range(TILES):
                    pool.wait_ge(s_hi, 2 * t + 2)
                    twice = values[:, t, :, 0:HD].unsqueeze(2).to_broadcast([P, HEADS, 2, HD])
                    pool.tensor_tensor(split_f[:, t % ZR, :, 1, :, :], twice, split_f[:, t % ZR, :, 0, :, :],
                                       ALU.subtract).then_inc(s_lo_f, 1)
                for u in masked:
                    pool.wait_ge(s_exp, u + 1)
                    tri = probs[:, u % UR, :, 0:P]
                    pool.affine_select(out=tri, in_=tri, compare_op=ALU.is_ge, fill=0.0, base=0,
                                       pattern=[[0, 2], [1, P]], channel_multiplier=-1).then_inc(s_mask, 1)

            @block.tensor
            def _(pe):
                for t in range(TILES):
                    pe.wait_ge(s_hi, 2 * t + 2)
                    pe.wait_ge(s_lo_m, t + 1)
                    pe.wait_ge(s_lo_f, t + 1)
                    if t >= 3:
                        pe.wait_ge(s_emov, t - 2)
                        pe.wait_ge(s_efix, 2 * (t - 2))
                    for split, bank, turned_tile in ((split_m, t % 3, s_tmov), (split_f, 3 + t % 3, s_tfix)):
                        for r in range(PAIRS):
                            mm = pe.transpose(turned[:, bank, r * P:(r + 1) * P],
                                              split[:, t % ZR, 2 * r:2 * r + 2].rearrange("p a i j e -> p (a i j e)"),
                                              pr.ident16[:])
                        mm.then_inc(turned_tile, 1)

                def turn_out(i):
                    pe.wait_ge(s_ocopy, i + 1)
                    for t in range(TPC):
                        mm = pe.transpose(heads_out[:, i % 2, t * P:(t + 1) * P], osb[:, i % 2, t * P:(t + 1) * P], pr.ident[:])
                    mm.then_inc(s_oturn, 1)

                def products(n):
                    c, g, kt = steps[n]
                    i = c * GROUPS + g
                    skip, w = span(c, kt)
                    if kt == 0 and i >= 2:
                        pe.wait_ge(s_added, i - 1)
                    pe.wait_ge(s_exp, 2 * n + 2)
                    if masks_by[2 * n + 1]:
                        pe.wait_ge(s_mask, masks_by[2 * n + 1])
                    for j in range(4):
                        mm = pe.matmul(heads_out[32 * j:32 * j + 32, i % 2, skip:CHUNK], values[:, kt, 4 * g + j, :],
                                       probs[:, (2 * n + j // 2) % UR, j % 2, 0:w], start=(kt == 0),
                                       stop=(kt == TPC * (c + 1) - 1), skip_group_check=True)
                    mm.then_inc(s_pv, 1)

                pe.wait_ge(s_emov, TILES)
                pe.wait_ge(s_efix, 2 * TILES)
                pe.wait_ge(s_zero, 2)
                turned_groups = 0
                for n, (c, g, kt) in enumerate(steps):
                    skip, w = span(c, kt)
                    q0 = c * CHUNK + skip
                    for a in range(2):
                        u = 2 * n + a
                        if u >= SR:
                            pe.wait_ge(s_exp, u - SR + 1)
                        for h in range(2):
                            head = 4 * g + 2 * a + h
                            mm = pe.matmul(scores[:, 2 * (u % SR) + h, 0:w], fixed[:, head, kt * P:(kt + 1) * P],
                                           moving[:, head // 2, q0:q0 + w], start=True, stop=True)
                        mm.then_inc(s_scores, 1)
                    if n >= 1:
                        products(n - 1)
                    if turned_groups < len(group_end) and n == group_end[turned_groups] + 2:
                        turn_out(turned_groups)
                        turned_groups += 1
                products(len(steps) - 1)
                for i in range(turned_groups, len(group_end)):
                    turn_out(i)


class NormedColumns:

    RING = 4

    def __init__(self, pr, st, b, sb, banks):
        self.pr, self.st, self.b, self.banks = pr, st, b, banks
        self.xn = sb(f"{st}_xn", [P, self.RING, D], F32)
        self.hi = sb(f"{st}_xhi", [P, KD, S], F32R)
        self.lo = sb(f"{st}_xlo", [P, KD, S], F32R)
        self.nsems = pr.norm_sems(st)
        self.s_xn, self.s_turn, self.s_hi, self.s_lo = pr.sems(st, "xn", "turn", "xhi", "xlo")

    def bank(self, i):
        return self.banks[:, i % 3, :].rearrange("p (k n) -> p k n", k=KD)

    def vector(self, dve, pooled=None):
        self.pr.norm_vector(dve, self.b, self.nsems)
        for i in range(TILES // 2 + 1):
            if i < TILES // 2:
                for t in (2 * i, 2 * i + 1):
                    if t >= self.RING:
                        dve.wait_ge(self.s_turn, (t - self.RING) // 2 + 1)
                        if pooled is not None:
                            dve.wait_ge(pooled, t - self.RING + 1)
                    dve.tensor_scalar(self.xn[:, t % self.RING, :], self.pr.x[:, self.b * TILES + t, :],
                                      self.pr.mv[:, t, 0:1], self.pr.rstd[:, t:t + 1], ALU.subtract, ALU.mult)\
                       .then_inc(self.s_xn, 1)
            if i >= 1:
                u = i - 1
                dve.wait_ge(self.s_hi, u + 1)
                cols = slice(2 * P * u, 2 * P * (u + 1))
                dve.tensor_tensor(self.lo[:, :, cols], self.bank(u), self.hi[:, :, cols].bitcast(F32), ALU.subtract)\
                   .then_inc(self.s_lo, 1)

    def scalar(self, act):
        self.pr.norm_scalar(act, self.nsems)
        for u in range(TILES // 2):
            act.wait_ge(self.s_turn, u + 1)
            act.activation(self.hi[:, :, 2 * P * u:2 * P * (u + 1)], self.bank(u), ACT.Copy).then_inc(self.s_hi, 1)

    def tensor(self, pe, each_tile=None):
        for u in range(TILES // 2):
            if u >= 3:
                pe.wait_ge(self.s_lo, u - 2)
            for t in (2 * u, 2 * u + 1):
                pe.wait_ge(self.s_xn, t + 1)
                for k in range(KD):
                    mm = pe.transpose(self.bank(u)[:, k, (t % 2) * P:(t % 2 + 1) * P],
                                      self.xn[:, t % self.RING, k * P:(k + 1) * P], self.pr.ident[:])
                if each_tile is not None and t % 2 == 0:
                    each_tile(t)
            mm.then_inc(self.s_turn, 1)
            if each_tile is not None:
                each_tile(2 * u + 1)


def split_product(pe, out, fixed_hi, fixed_lo, moving_hi, moving_lo, first, last):
    pe.matmul(out, fixed_hi, moving_hi, start=first, stop=False)
    pe.matmul(out, fixed_hi, moving_lo, start=False, stop=False)
    return pe.matmul(out, fixed_lo, moving_hi, start=False, stop=last)


def add_columns(pr, st, b, turn_bank):
    s_turned, s_added = pr.sems(st, "result_turned", "result_added")

    def tensor(pe, c, half, result, s_result):
        n = c * (TPC // 2) + half
        pe.wait_ge(s_result, KD * (c + 1))
        if n >= 1:
            pe.wait_ge(s_added, n)
        for t in range(2):
            for k in range(KD):
                q = (2 * half + t) * P
                mm = pe.transpose(turn_bank[:, (t * KD + k) * P:(t * KD + k + 1) * P], result[:, k, q:q + P], pr.ident[:])
        mm.then_inc(s_turned, 1)

    def vector(dve, c, half):
        n = c * (TPC // 2) + half
        dve.wait_ge(s_turned, n + 1)
        xv = pr.x[:, b * TILES + c * TPC + 2 * half:b * TILES + c * TPC + 2 * half + 2, :]
        dve.tensor_tensor(xv, xv, turn_bank[:].rearrange("p (t d) -> p t d", t=2), ALU.add).then_inc(s_added, 1)

    return tensor, vector, s_turned, s_added


def mixture(pr, layer, b):
    nc = pr.nc
    st = f"f{layer}{b}"
    with ExitStack() as ctx:
        sb, ps = pr.sb(ctx), pr.ps(ctx)
        raw1 = sb(f"{st}_raw1", [P, TOPK, KD, F], F32)
        raw2 = sb(f"{st}_raw2", [P, TOPK, FT, D], F32)
        w1h = sb(f"{st}_w1h", [P, TOPK, KD, F], F32R)
        w1l = sb(f"{st}_w1l", [P, TOPK, KD, F], F32R)
        w2h = sb(f"{st}_w2h", [P, TOPK, FT, D], F32R)
        w2l = sb(f"{st}_w2l", [P, TOPK, FT, D], F32R)
        HR = 3
        gel = sb(f"{st}_gelu", [P, HR, CHUNK], F32)
        hh = sb(f"{st}_hh", [P, HR, CHUNK], F32R)
        hl = sb(f"{st}_hl", [P, HR, CHUNK], F32R)
        ysb = sb(f"{st}_y", [P, KD, CHUNK], F32)
        BR = TOPK * (FT + KD)
        brow = sb(f"{st}_brow", [BR, P], F32)
        bcol = sb(f"{st}_bcol", [P, BR], F32)
        b2w = sb(f"{st}_b2w", [P, 2, KD], F32)
        pooled = sb(f"{st}_pooled", [P, KD], F32)
        logits = sb(f"{st}_logits", [1, E], F32)
        best = sb(f"{st}_best", [1, 8], F32)
        best_i = sb(f"{st}_best_i", [1, 8], U32)
        gate = sb(f"{st}_gate", [1, 8], F32)
        gates = sb(f"{st}_gates", [P, TOPK], F32)
        hps = ps(f"{st}_h", [P, 3, CHUNK], F32)
        yps = ps(f"{st}_ypsum", [P, 2 * KD, CHUNK], F32)
        misc = ps(f"{st}_misc", [P, CHUNK], F32)
        cols = NormedColumns(pr, st, b, sb, hps)

        (s_sum, s_pooled, s_logit, s_logits, s_best, s_besti, s_diff, s_e, s_gate, s_spread, s_gates,
         s_b2w, s_bturn, s_bcol) = pr.sems(
            st, "sum", "pooled", "logit", "logits", "best", "besti", "diff", "e", "gate", "spread", "gates",
            "b2w", "bturn", "bcol")
        s_braw, s_wh, s_wl, s_h, s_gelu, s_hh, s_hl, s_used, s_y = pr.sems(
            st, "braw", "wh", "wl", "h", "gelu", "hh", "hl", "used", "y")
        s_raw = pr.sems(st, "raw1_0", "raw2_0", "raw1_1", "raw2_1")
        add_tensor, add_vector, s_rturned, s_added = add_columns(pr, st, b, misc)

        steps = [(c, e, j) for c in range(CHUNKS) for e in range(TOPK) for j in range(FT)]
        parts = []
        for e in range(TOPK):
            for w, raw, hi, lo in ((0, raw1, w1h, w1l), (1, raw2, w2h, w2l)):
                flat = [m[:, e].rearrange("p a n -> p (a n)") for m in (raw, hi, lo)]
                for i in range(4):
                    parts.append((s_raw[2 * e + w], *[m[:, 512 * i:512 * i + 512] for m in flat]))

        with nc.Block() as block:
            @block.sync
            def _(sp):
                sp.wait_ge(s_besti, 1)
                for e in range(TOPK):
                    n = sp.value_load(best_i[0:1, e:e + 1], min_val=0, max_val=E - 1)
                    sp.dma_start(raw1[:, e], pr.W1[bass.ds(n, 1)].rearrange("o (k p) f -> p (o k) f", p=P)).then_inc(s_raw[2 * e], 16)
                    sp.dma_start(brow[FT * e:FT * e + FT, :], pr.b1[bass.ds(n, 1)].rearrange("o (j p) -> (o j) p", p=P)).then_inc(s_braw, 16)
                    o = TOPK * FT + KD * e
                    sp.dma_start(brow[o:o + KD, :], pr.b2[bass.ds(n, 1)].rearrange("o (k p) -> (o k) p", p=P)).then_inc(s_braw, 16)
                    sp.dma_start(raw2[:, e], pr.W2[bass.ds(n, 1)].rearrange("o (j p) d -> p (o j) d", p=P)).then_inc(s_raw[2 * e + 1], 16)

            @block.tensor
            def _(pe):
                def sum_tile(t):
                    for k in range(KD):
                        mm = pe.matmul(yps[:, k, 0:1], cols.xn[:, t % cols.RING, k * P:(k + 1) * P], pr.ones[:, 0:1],
                                       start=(t == 0), stop=(t == TILES - 1))
                    mm.then_inc(s_sum, 1)
                cols.tensor(pe, sum_tile)
                pe.wait_ge(s_pooled, 1)
                for k in range(KD):
                    mm = pe.matmul(misc[0:1, 0:E], pooled[:, k:k + 1], pr.wr[:, k, :], start=(k == 0), stop=(k == KD - 1))
                mm.then_inc(s_logit, 1)
                pe.wait_ge(s_gate, 3)
                pe.wait_ge(s_logits, 1)
                pe.matmul(misc[:, 0:TOPK], pr.ones[0:1, :], gate[0:1, 3:3 + TOPK], start=True, stop=True).then_inc(s_spread, 1)
                pe.wait_ge(s_braw, 4 * 16)
                pe.wait_ge(s_gates, 1)
                pe.transpose(misc[:, 0:BR], brow[:], pr.ident[0:BR, 0:BR]).then_inc(s_bturn, 1)
                pe.wait_ge(s_bcol, 1)
                pe.wait_ge(cols.s_lo, TILES // 2)

                def up(n):
                    c, e, j = steps[n]
                    if n < TOPK * FT and j == 0:
                        pe.wait_ge(s_wh, 8 * e + 4)
                        pe.wait_ge(s_wl, 8 * e + 4)
                    if n >= 3:
                        pe.wait_ge(s_gelu, n - 2)
                    for k in range(KD):
                        mm = split_product(pe, hps[:, n % 3, :], w1h[:, e, k, j * P:(j + 1) * P], w1l[:, e, k, j * P:(j + 1) * P],
                                           cols.hi[:, k, c * CHUNK:(c + 1) * CHUNK], cols.lo[:, k, c * CHUNK:(c + 1) * CHUNK],
                                           k == 0, k == KD - 1)
                    mm.then_inc(s_h, 1)

                def down(n):
                    c, e, j = steps[n]
                    if n < TOPK * FT and j == 0:
                        pe.wait_ge(s_wh, 8 * e + 8)
                        pe.wait_ge(s_wl, 8 * e + 8)
                    if e == 0 and j == 0 and c >= 2:
                        pe.wait_ge(s_y, KD * (c - 1))
                    pe.wait_ge(s_hh, n + 1)
                    pe.wait_ge(s_hl, n + 1)
                    for k in range(KD):
                        mm = split_product(pe, yps[:, KD * (c % 2) + k, :], w2h[:, e, j, k * P:(k + 1) * P],
                                           w2l[:, e, j, k * P:(k + 1) * P], hh[:, n % HR, :], hl[:, n % HR, :],
                                           e == 0 and j == 0, e == TOPK - 1 and j == FT - 1)
                    mm.then_inc(s_used, 1)

                for n in range(len(steps) + 2):
                    if n < len(steps):
                        up(n)
                    if n >= 2:
                        down(n - 2)
                    c, at = divmod(n, TOPK * FT)
                    if 1 <= c < CHUNKS and at in (4, 6):
                        add_tensor(pe, c - 1, (at - 4) // 2, ysb, s_y)
                for half in range(2):
                    add_tensor(pe, CHUNKS - 1, half, ysb, s_y)

            @block.scalar
            def _(act):
                cols.scalar(act)
                act.wait_ge(s_diff, 1)
                act.activation(gate[0:1, 1:2], gate[0:1, 0:1], ACT.Exp).then_inc(s_e, 1)
                for i, (arrived, raw, hi, lo) in enumerate(parts):
                    act.wait_ge(arrived, 16)
                    act.activation(hi, raw, ACT.Copy).then_inc(s_wh, 1)
                act.wait_ge(s_bcol, 1)
                for n, (c, e, j) in enumerate(steps):
                    act.wait_ge(s_h, n + 1)
                    if n >= HR:
                        act.wait_ge(s_hl, n - HR + 1)
                    act.activation(gel[:, n % HR, :], hps[:, n % 3, :], ACT.Gelu, bias=bcol[:, FT * e + j:FT * e + j + 1])\
                       .then_inc(s_gelu, 1)

            @block.vector
            def _(dve):
                cols.vector(dve, s_sum)
                dve.wait_ge(s_sum, TILES)
                dve.tensor_scalar(pooled[:], yps[:, 0:KD, 0], 1.0 / S, None, ALU.mult).then_inc(s_pooled, 1)
                dve.wait_ge(s_logit, 1)
                dve.tensor_copy(logits[:], misc[0:1, 0:E]).then_inc(s_logits, 1)
                dve.wait_ge(s_logits, 1)
                dve.max(best[:], logits[:]).then_inc(s_best, 1)
                dve.wait_ge(s_best, 1)
                dve.max_index(best_i[:], best[:], logits[:]).then_inc(s_besti, 1)
                dve.tensor_tensor(gate[0:1, 0:1], best[0:1, 1:2], best[0:1, 0:1], ALU.subtract).then_inc(s_diff, 1)
                dve.wait_ge(s_e, 1)
                dve.tensor_scalar(gate[0:1, 2:3], gate[0:1, 1:2], 1.0, None, ALU.add).then_inc(s_gate, 1)
                dve.wait_ge(s_gate, 1)
                dve.reciprocal(gate[0:1, 3:4], gate[0:1, 2:3]).then_inc(s_gate, 1)
                dve.wait_ge(s_gate, 2)
                dve.tensor_tensor(gate[0:1, 4:5], gate[0:1, 3:4], gate[0:1, 1:2], ALU.mult).then_inc(s_gate, 1)
                dve.wait_ge(s_spread, 1)
                dve.tensor_copy(gates[:], misc[:, 0:TOPK]).then_inc(s_gates, 1)

                def low_part(i):
                    arrived, raw, hi, lo = parts[i]
                    dve.wait_ge(s_wh, i + 1)
                    dve.tensor_tensor(lo, raw, hi.bitcast(F32), ALU.subtract).then_inc(s_wl, 1)
                for i in range(4):
                    low_part(i)
                dve.wait_ge(s_bturn, 1)
                dve.tensor_copy(bcol[:], misc[:, 0:BR]).then_inc(s_bcol, 1)
                dve.wait_ge(s_bcol, 1)
                dve.wait_ge(s_gates, 1)
                o = TOPK * FT
                dve.tensor_scalar(b2w[:, 0, :], bcol[:, o:o + KD], gates[:, 0:1], None, ALU.mult).then_inc(s_b2w, 1)
                dve.wait_ge(s_b2w, 1)
                dve.scalar_tensor_tensor(out=b2w[:, 1, :], in0=bcol[:, o + KD:o + 2 * KD], scalar=gates[:, 1:2],
                                         in1=b2w[:, 0, :], op0=ALU.mult, op1=ALU.add).then_inc(s_b2w, 1)
                for i in range(4, len(parts)):
                    low_part(i)

                def result(c):
                    dve.wait_ge(s_used, (c + 1) * TOPK * FT)
                    if c == 0:
                        dve.wait_ge(s_b2w, 2)
                    else:
                        dve.wait_ge(s_rturned, (TPC // 2) * c)
                    for k in range(KD):
                        dve.tensor_scalar(ysb[:, k, :], yps[:, KD * (c % 2) + k, :], b2w[:, 1, k:k + 1], None, ALU.add)\
                           .then_inc(s_y, 1)

                for n, (c, e, j) in enumerate(steps):
                    dve.wait_ge(s_gelu, n + 1)
                    if n >= HR:
                        dve.wait_ge(s_used, n - HR + 1)
                    dve.tensor_scalar(hh[:, n % HR, :], gel[:, n % HR, :], gates[:, e:e + 1], None, ALU.mult).then_inc(s_hh, 1)
                    dve.wait_ge(s_hh, n + 1)
                    dve.scalar_tensor_tensor(out=hl[:, n % HR, :], in0=gel[:, n % HR, :], scalar=gates[:, e:e + 1],
                                             in1=hh[:, n % HR, :].bitcast(F32), op0=ALU.mult, op1=ALU.subtract).then_inc(s_hl, 1)
                    at = n % (TOPK * FT)
                    if c >= 1 and at == 2:
                        result(c - 1)
                    if c >= 1 and at in (4, 6):
                        add_vector(dve, c - 1, (at - 4) // 2)
                result(CHUNKS - 1)
                for half in range(2):
                    add_vector(dve, CHUNKS - 1, half)


class DistanceWeights:

    def __init__(self, pr, ctx):
        nc = pr.nc
        sb = pr.sb(ctx)
        self.hi, self.lo = {}, {}
        for name in ("q", "k", "vo"):
            self.hi[name] = sb(f"w{name}_hi", [P, KD, D], F32R)
            self.lo[name] = sb(f"w{name}_lo", [P, KD, D], F32R)
        s_w, s_vturn, s_vcol, s_vo, s_bvo, s_vo32, s_hi, s_lo, s_bias = pr.sems(
            "dw", "w", "vturn", "vcol", "vo", "bvo", "vo32", "hi", "lo", "bias")
        with ExitStack() as tmp:
            tsb, ps = pr.sb(tmp), pr.ps(tmp)
            raw = {n: tsb(f"w{n}_raw", [P, KD, D], F32) for n in ("q", "k", "v", "o", "vo")}
            vcol = tsb("wv_turned", [P, KD, D], F32)
            turn = ps("dw_turn", [P, KD, D], F32)
            prod = ps("dw_prod", [P, KD, D], F32)
            bias = ps("dw_bias", [P, KD], F32)
            block = tmp.enter_context(nc.Block())

            @block.sync
            def _(sp):
                for n, w in (("v", pr.Wv), ("o", pr.Wo), ("q", pr.Wq), ("k", pr.Wk)):
                    sp.dma_start(raw[n][:], w.rearrange("(k p) n -> p k n", p=P)).then_inc(s_w, 16)

            @block.tensor
            def _(pe):
                pe.wait_ge(s_w, 64)
                for r in range(KD):
                    for k in range(KD):
                        mm = pe.transpose(turn[:, k, r * P:(r + 1) * P], raw["v"][:, r, k * P:(k + 1) * P], pr.ident[:])
                mm.then_inc(s_vturn, 1)
                pe.wait_ge(s_vcol, 1)
                for r in range(KD):
                    for k in range(KD):
                        mm = pe.matmul(prod[:, r, :], vcol[:, k, r * P:(r + 1) * P], raw["o"][:, k, :],
                                       start=(k == 0), stop=(k == KD - 1))
                mm.then_inc(s_vo, 1)
                for m in range(KD):
                    for k in range(KD):
                        mm = pe.matmul(bias[:, m:m + 1], raw["o"][:, k, m * P:(m + 1) * P], pr.bias_b[:, 2, k:k + 1],
                                       start=(k == 0), stop=(k == KD - 1))
                mm.then_inc(s_bvo, 1)

            @block.vector
            def _(dve):
                dve.wait_ge(s_vturn, 1)
                dve.tensor_copy(vcol[:], turn[:]).then_inc(s_vcol, 1)
                dve.wait_ge(s_vo, 1)
                dve.tensor_copy(raw["vo"][:], prod[:]).then_inc(s_vo32, 1)
                dve.wait_ge(s_vo32, 1)
                dve.wait_ge(s_w, 64)
                for n in ("q", "k", "vo"):
                    dve.tensor_copy(self.hi[n][:], raw[n][:]).then_inc(s_hi, 1)
                for i, n in enumerate(("q", "k", "vo")):
                    dve.wait_ge(s_hi, i + 1)
                    dve.tensor_tensor(self.lo[n][:], raw[n][:], self.hi[n][:].bitcast(F32), ALU.subtract).then_inc(s_lo, 1)
                dve.wait_ge(s_bvo, 1)
                dve.tensor_tensor(pr.bvo[:], bias[:], pr.bias_b[:, 3, :], ALU.add).then_inc(s_bias, 1)


def distance_weights(pr, ctx):
    return DistanceWeights(pr, ctx)


def distance_attention(pr, b, w):
    nc = pr.nc
    st = f"b{b}"
    with ExitStack() as ctx:
        sb, ps = pr.sb(ctx), pr.ps(ctx)
        hi = {n: sb(f"{st}_{n}hi", [P, KD, S], F32R) for n in "qk"}
        lo = {n: sb(f"{st}_{n}lo", [P, KD, S], F32R) for n in "qk"}
        vhi = sb(f"{st}_vhi", [P, TILES, D], F32R)
        vlo = sb(f"{st}_vlo", [P, TILES, D], F32R)
        qsq = sb(f"{st}_qsq", [P, S], F32)
        nksq = sb(f"{st}_nksq", [P, TILES], F32)
        banks = ps(f"{st}_banks", [P, 3, CHUNK], F32)
        outs = ps(f"{st}_outs", [P, 2 * KD, CHUNK], F32)
        misc = ps(f"{st}_misc", [P, CHUNK], F32)

        with ExitStack() as part:
            psb = pr.sb(part)
            cols = NormedColumns(pr, st, b, psb, banks)
            qk32 = psb(f"{st}_qk32", [P, 2, KD, CHUNK], F32)
            square = psb(f"{st}_square", [P, 2, KD, CHUNK], F32)
            s_v, s_vhi, s_vlo, s_p, s_p32, s_phi, s_plo, s_sq, s_len, s_lenc = pr.sems(
                st, "v", "vhi", "vlo", "p", "p32", "phi", "plo", "sq", "len", "lenc")
            tasks = [(n, c) for n in "kq" for c in range(CHUNKS)]
            with nc.Block() as block:
                @block.tensor
                def _(pe):
                    cols.tensor(pe)
                    for u in range(TILES // 2):
                        pe.wait_ge(cols.s_lo, min(u + TILES // 2 - 2, TILES // 2))
                        if u >= 3:
                            pe.wait_ge(s_vlo, u - 2)
                        for t in (2 * u, 2 * u + 1):
                            for k in range(KD):
                                tok = slice(t * P, (t + 1) * P)
                                o = banks[:, (u + 2) % 3, (t % 2) * D:(t % 2 + 1) * D]
                                mm = split_product(pe, o, cols.hi[:, k, tok], cols.lo[:, k, tok], w.hi["vo"][:, k, :],
                                                   w.lo["vo"][:, k, :], k == 0, k == KD - 1)
                        mm.then_inc(s_v, 1)

                    def lengths(i):
                        n, c = tasks[i]
                        pe.wait_ge(s_sq, KD * (i + 1))
                        if i >= 1:
                            pe.wait_ge(s_lenc, i)
                        if n == "q":
                            for m in range(KD):
                                mm = pe.matmul(misc[:], pr.ones[:], square[:, i % 2, m, :], start=(m == 0), stop=(m == KD - 1))
                        else:
                            for t in range(TPC):
                                for m in range(KD):
                                    mm = pe.matmul(misc[:, t:t + 1], square[:, i % 2, m, t * P:(t + 1) * P], pr.ones[:, 0:1],
                                                   start=(m == 0), stop=(m == KD - 1))
                        mm.then_inc(s_len, 1)

                    for i, (n, c) in enumerate(tasks):
                        for m in range(KD):
                            j = KD * i + m
                            if j >= 4:
                                pe.wait_ge(s_p32, j - 3)
                            for k in range(KD):
                                mm = split_product(pe, outs[:, j % 4, :], w.hi[n][:, k, m * P:(m + 1) * P],
                                                   w.lo[n][:, k, m * P:(m + 1) * P], cols.hi[:, k, c * CHUNK:(c + 1) * CHUNK],
                                                   cols.lo[:, k, c * CHUNK:(c + 1) * CHUNK], k == 0, k == KD - 1)
                            mm.then_inc(s_p, 1)
                        if i >= 1:
                            lengths(i - 1)
                    lengths(len(tasks) - 1)

                @block.scalar
                def _(act):
                    cols.scalar(act)
                    for u in range(TILES // 2):
                        act.wait_ge(s_v, u + 1)
                        act.activation(vhi[:, 2 * u:2 * u + 2, :], banks[:, (u + 2) % 3, :].rearrange("p (t d) -> p t d", t=2),
                                       ACT.Copy).then_inc(s_vhi, 1)
                    for i, (n, c) in enumerate(tasks):
                        for m in range(KD):
                            j = KD * i + m
                            act.wait_ge(s_p, j + 1)
                            if i >= 2:
                                act.wait_ge(s_sq, j - 3)
                                act.wait_ge(s_plo, j - 3)
                            act.activation(qk32[:, i % 2, m, :], outs[:, j % 4, :], ACT.Identity,
                                           bias=pr.bias_b[:, 0 if n == "q" else 1, m:m + 1]).then_inc(s_p32, 1)

                @block.gpsimd
                def _(pool):
                    for i in range(len(tasks)):
                        for m in range(KD):
                            pool.wait_ge(s_p32, KD * i + m + 1)
                            if i >= 2:
                                pool.wait_ge(s_len, i - 1)
                            t32 = qk32[:, i % 2, m, :]
                            pool.tensor_tensor(square[:, i % 2, m, :], t32, t32, ALU.mult).then_inc(s_sq, 1)

                @block.vector
                def _(dve):
                    cols.vector(dve)
                    for u in range(TILES // 2):
                        dve.wait_ge(s_vhi, u + 1)
                        dve.tensor_tensor(vlo[:, 2 * u:2 * u + 2, :], banks[:, (u + 2) % 3, :].rearrange("p (t d) -> p t d", t=2),
                                          vhi[:, 2 * u:2 * u + 2, :].bitcast(F32), ALU.subtract).then_inc(s_vlo, 1)

                    def read_lengths(i):
                        n, c = tasks[i]
                        dve.wait_ge(s_len, i + 1)
                        if n == "q":
                            dve.tensor_copy(qsq[:, c * CHUNK:(c + 1) * CHUNK], misc[:]).then_inc(s_lenc, 1)
                        else:
                            dve.tensor_scalar(nksq[:, c * TPC:(c + 1) * TPC], misc[:, 0:TPC], -1.0, None, ALU.mult).then_inc(s_lenc, 1)

                    for i, (n, c) in enumerate(tasks):
                        for m in range(KD):
                            j = KD * i + m
                            dve.wait_ge(s_p32, j + 1)
                            cut = slice(c * CHUNK, (c + 1) * CHUNK)
                            dve.tensor_copy(hi[n][:, m, cut], qk32[:, i % 2, m, :]).then_inc(s_phi, 1)
                            dve.wait_ge(s_phi, j + 1)
                            dve.tensor_tensor(lo[n][:, m, cut], qk32[:, i % 2, m, :], hi[n][:, m, cut].bitcast(F32),
                                              ALU.subtract).then_inc(s_plo, 1)
                        if i >= 1:
                            read_lengths(i - 1)
                    read_lengths(len(tasks) - 1)

        with ExitStack() as part:
            psb = pr.sb(part)
            R = 3
            dist = psb(f"{st}_dist", [P, R, CHUNK], F32)
            score = psb(f"{st}_score", [P, R, CHUNK], F32)
            p32 = psb(f"{st}_p32", [P, R, CHUNK], F32)
            phi = psb(f"{st}_phi", [P, R, CHUNK], F32R)
            plo = psb(f"{st}_plo", [P, R, CHUNK], F32R)
            psum_acc = psb(f"{st}_psum_acc", [P, 2, CHUNK], F32)
            rden = psb(f"{st}_rden", [P, CHUNK], F32)
            ysb = psb(f"{st}_y", [P, KD, CHUNK], F32)
            s_qk, s_dist, s_score, s_p32, s_phi, s_plo, s_acc, s_pv, s_den, s_rden, s_on, s_y = pr.sems(
                st, "qk", "dist", "score", "prob", "probhi", "problo", "acc", "pv", "den", "rden", "on", "y")
            add_tensor, add_vector, s_rturned, s_added = add_columns(pr, st, b, misc)
            steps = [(c, kt) for c in range(CHUNKS) for kt in range(TILES)]

            def summed(n):
                return (TILES - 1) * (n // TILES) + max(n % TILES, 1)

            with nc.Block() as block:
                @block.tensor
                def _(pe):
                    def scores(n):
                        c, kt = steps[n]
                        if n >= 3:
                            pe.wait_ge(s_dist, n - 2)
                        for k in range(KD):
                            mm = split_product(pe, banks[:, n % 3, :], hi["k"][:, k, kt * P:(kt + 1) * P],
                                               lo["k"][:, k, kt * P:(kt + 1) * P], hi["q"][:, k, c * CHUNK:(c + 1) * CHUNK],
                                               lo["q"][:, k, c * CHUNK:(c + 1) * CHUNK], k == 0, k == KD - 1)
                        mm.then_inc(s_qk, 1)

                    def values(n):
                        c, kt = steps[n]
                        if kt == 0 and c >= 2:
                            pe.wait_ge(s_on, KD * (c - 1))
                        pe.wait_ge(s_phi, n + 1)
                        pe.wait_ge(s_plo, n + 1)
                        for m in range(KD):
                            mm = split_product(pe, outs[:, KD * (c % 2) + m, :], vhi[:, kt, m * P:(m + 1) * P],
                                               vlo[:, kt, m * P:(m + 1) * P], phi[:, n % R, :], plo[:, n % R, :],
                                               kt == 0, kt == TILES - 1)
                        mm.then_inc(s_pv, 1)

                    def denominator(c):
                        pe.wait_ge(s_acc, (TILES - 1) * (c + 1))
                        if c >= 1:
                            pe.wait_ge(s_added, (TPC // 2) * c)
                        pe.matmul(misc[:], pr.ones[:], psum_acc[:, c % 2, :], start=True, stop=True).then_inc(s_den, 1)

                    LAG = 2
                    for n in range(len(steps) + LAG):
                        if n < len(steps):
                            scores(n)
                        if n >= LAG:
                            values(n - LAG)
                        c, at = divmod(n, TILES)
                        if 1 <= c < CHUNKS and at == 3:
                            denominator(c - 1)
                        if 1 <= c < CHUNKS and at in (7, 9):
                            add_tensor(pe, c - 1, (at - 7) // 2, ysb, s_y)
                    denominator(CHUNKS - 1)
                    for half in range(2):
                        add_tensor(pe, CHUNKS - 1, half, ysb, s_y)

                @block.scalar
                def _(act):
                    def second(n):
                        act.wait_ge(s_score, n + 1)
                        if n >= R:
                            act.wait_ge(s_plo, n - R + 1)
                            act.wait_ge(s_acc, summed(n - R))
                        act.activation(p32[:, n % R, :], score[:, n % R, :], ACT.Exp).then_inc(s_p32, 1)
                    for n, (c, kt) in enumerate(steps):
                        act.wait_ge(s_dist, n + 1)
                        if n >= R:
                            act.wait_ge(s_p32, n - R + 1)
                        act.activation(score[:, n % R, :], dist[:, n % R, :], ACT.Exp, scale=-1.0,
                                       bias=nksq[:, kt:kt + 1]).then_inc(s_score, 1)
                        if n >= 1:
                            second(n - 1)
                    second(len(steps) - 1)

                @block.gpsimd
                def _(pool):
                    done = 0
                    for n, (c, kt) in enumerate(steps):
                        if kt == 0:
                            continue
                        pool.wait_ge(s_p32, n + 1)
                        acc = psum_acc[:, c % 2, :]
                        if kt == 1:
                            if c >= 2:
                                pool.wait_ge(s_den, c - 1)
                            pool.tensor_tensor(acc, p32[:, (n - 1) % R, :], p32[:, n % R, :], ALU.add).then_inc(s_acc, 1)
                        else:
                            pool.wait_ge(s_acc, done)
                            pool.tensor_tensor(acc, acc, p32[:, n % R, :], ALU.add).then_inc(s_acc, 1)
                        done += 1

                @block.vector
                def _(dve):
                    def halves(n):
                        dve.wait_ge(s_p32, n + 1)
                        if n >= R:
                            dve.wait_ge(s_pv, n - R + 1)
                        dve.tensor_copy(phi[:, n % R, :], p32[:, n % R, :]).then_inc(s_phi, 1)
                        dve.wait_ge(s_phi, n + 1)
                        dve.tensor_tensor(plo[:, n % R, :], p32[:, n % R, :], phi[:, n % R, :].bitcast(F32), ALU.subtract)\
                           .then_inc(s_plo, 1)

                    def result(c):
                        dve.wait_ge(s_den, c + 1)
                        dve.reciprocal(rden[:], misc[:]).then_inc(s_rden, 1)
                        dve.wait_ge(s_rden, c + 1)
                        dve.wait_ge(s_pv, TILES * (c + 1))
                        if c >= 1:
                            dve.wait_ge(s_rturned, (TPC // 2) * c)
                        for m in range(KD):
                            dve.tensor_tensor(ysb[:, m, :], outs[:, KD * (c % 2) + m, :], rden[:], ALU.mult).then_inc(s_on, 1)
                        for m in range(KD):
                            dve.wait_ge(s_on, KD * c + m + 1)
                            dve.tensor_scalar(ysb[:, m, :], ysb[:, m, :], pr.bvo[:, m:m + 1], None, ALU.add).then_inc(s_y, 1)

                    for n in range(len(steps) + 1):
                        if n < len(steps):
                            c, kt = steps[n]
                            dve.wait_ge(s_qk, n + 1)
                            if n >= R:
                                dve.wait_ge(s_score, n - R + 1)
                            dve.scalar_tensor_tensor(out=dist[:, n % R, :], in0=banks[:, n % 3, :], scalar=-2.0,
                                                     in1=qsq[:, c * CHUNK:(c + 1) * CHUNK], op0=ALU.mult, op1=ALU.add)\
                               .then_inc(s_dist, 1)
                        if n >= 1:
                            halves(n - 1)
                        c, at = divmod(n, TILES)
                        if 1 <= c < CHUNKS and at == 4:
                            result(c - 1)
                        if 1 <= c < CHUNKS and at in (7, 9):
                            add_vector(dve, c - 1, (at - 7) // 2)
                    result(CHUNKS - 1)
                    for half in range(2):
                        add_vector(dve, CHUNKS - 1, half)


def finish(pr):
    s_out = pr.s_out
    with pr.nc.Block() as block:
        @block.sync
        def _(sp):
            for b in range(NB):
                sp.dma_start(pr.out_d[b].rearrange("(t p) d -> p t d", p=P), pr.x[:, b * TILES:(b + 1) * TILES, :]).then_inc(s_out, 16)
            sp.wait_ge(s_out, 32)


def hybrid_block(nc, *args):
    with ExitStack() as ctx:
        pr = Program(nc, ctx, args)
        setup(pr)
        for b in range(NB):
            head_attention(pr, b)
            pr.end_stage()
        for b in range(NB):
            mixture(pr, 0, b)
            pr.end_stage()
        with ExitStack() as weights_ctx:
            w = DistanceWeights(pr, weights_ctx)
            for b in range(NB):
                distance_attention(pr, b, w)
                pr.end_stage()
        for b in range(NB):
            mixture(pr, 1, b)
            pr.end_stage()
        finish(pr)


_INS = ["L0_attn_a_x", "L0_attn_b_Wq", "L0_attn_b_bq", "L0_attn_b_Wk", "L0_attn_b_bk", "L0_attn_b_Wv",
        "L0_attn_b_bv", "L0_attn_b_Wo", "L0_attn_b_bo", "L0_ffn_Wr", "L0_ffn_W1", "L0_ffn_b1", "L0_ffn_W2", "L0_ffn_b2"]


def kernel(**inputs):
    import concourse.bacc as _bacc
    from concourse.bass_utils import run_bass_kernel_spmd as _run

    nc = _bacc.Bacc("TRN2", target_bir_lowering=False, num_devices=1)
    arrays, args = {}, []
    for name in _INS:
        a = np.ascontiguousarray(inputs[name])
        arrays[f"in_{name}"] = a
        args.append(nc.dram_tensor(f"in_{name}", a.shape, mybir.dt.from_np(a.dtype), kind="ExternalInput").ap())
    args.append(nc.dram_tensor("out_0", (NB, S, D), F32, kind="ExternalOutput").ap())
    hybrid_block(nc, *args)
    r = _run(nc, [arrays], core_ids=[0])
    return r.results[0]["out_0"]
```

```python
from contextlib import ExitStack

import numpy as np

import concourse.bass as bass
from concourse import mybir

F32 = mybir.dt.float32
F32R = mybir.dt.float32r
F16 = mybir.dt.float16
U32 = mybir.dt.uint32
I32 = mybir.dt.int32
ALU = mybir.AluOpType
ACT = mybir.ActivationFunctionType
AX = mybir.AxisListType

P = 128
EPS = 1e-5
NB, S, D = 2, 2048, 256
TILES = S // P
CHUNK = 512
CHUNKS = S // CHUNK
TPC = CHUNK // P
KD = D // P
HEADS, HD = 16, 16
PAIRS = HEADS // 2
GROUPS = HEADS // 4
E, F = 8, 1024
FT = F // P
TOPK = 2


class Program:

    def __init__(self, nc, ctx, args):
        self.nc, self.stage_sems = nc, []
        self.s_out = nc.alloc_semaphore(name="out_stored")
        self.s_x = [nc.alloc_semaphore(name=f"x_loaded{b}") for b in range(NB)]
        (self.x_d, self.Wq, self.bq, self.Wk, self.bk, self.Wv, self.bv, self.Wo, self.bo,
         self.Wr, self.W1, self.b1, self.W2, self.b2, self.out_d) = args
        sb = self.sb(ctx)
        self.x = sb("x", [P, NB * TILES, D], F32)
        self.ident = sb("ident", [P, P], F32)
        self.ident16 = sb("ident16", [P, P], F16)
        self.ones = sb("ones", [P, P], F32)
        self.wr = sb("wr", [P, KD, E], F32)
        self.stats = sb("stats", [P, TILES, 6], F32)
        self.mv = sb("mv", [P, NB, TILES, 2], F32)
        self.rstd = sb("rstd", [P, NB, TILES], F32)
        self.vare = sb("vare", [P, TILES], F32)
        self.newton = sb("newton", [P, 2, TILES], F32)
        self.bias_b = sb("bias_b", [P, 4, KD], F32)
        self.bvo = sb("bvo", [P, D], F32)

    def sb(self, ctx):
        return lambda name, shape, dt: ctx.enter_context(self.nc.sbuf_tensor(name, shape, dt))

    def ps(self, ctx):
        return lambda name, shape, dt: ctx.enter_context(self.nc.psum_tensor(name, shape, dt))

    def sems(self, stage, *names):
        made = [self.nc.alloc_semaphore(name=f"{stage}_{n}") for n in names]
        self.stage_sems += made
        return made

    def end_stage(self):
        self.nc.clear_and_free_semaphores(self.stage_sems)
        self.nc.all_engine_barrier()
        self.stage_sems = []


class Norm:

    CHAIN = 11

    def __init__(self, pr, st, b):
        self.pr, self.b = pr, b
        self.s_stats, self.s_aggr, self.s_chain = pr.sems(st, f"stats{b}", f"aggr{b}", f"newton{b}")

    def stats(self, dve, t):
        dve.bn_stats(self.pr.stats[:, t, :], self.pr.x[:, self.b * TILES + t, :]).then_inc(self.s_stats, 1)

    def rest(self, dve):
        pr, b = self.pr, self.b
        for t in range(TILES):
            dve.wait_ge(self.s_stats, t + 1)
            dve.bn_aggr(pr.mv[:, b, t, :], pr.stats[:, t, :]).then_inc(self.s_aggr, 1)
        dve.wait_ge(self.s_aggr, TILES)
        v, y, a, c = pr.vare[:], pr.rstd[:, b, :], pr.newton[:, 0, :], pr.newton[:, 1, :]
        dve.tensor_scalar(v, pr.mv[:, b, :, 1], EPS, None, ALU.add).then_inc(self.s_chain, 1)
        dve.wait_ge(self.s_chain, 1)
        dve.tensor_scalar(y.bitcast(I32), v.bitcast(I32), -0.5, float(0x5F3759DF), ALU.mult, ALU.add)\
           .then_inc(self.s_chain, 1)
        for i in range(3):
            dve.wait_ge(self.s_chain, 3 * i + 2)
            dve.scalar_tensor_tensor(out=a, in0=v, scalar=-0.5, in1=y, op0=ALU.mult, op1=ALU.mult).then_inc(self.s_chain, 1)
            dve.wait_ge(self.s_chain, 3 * i + 3)
            dve.tensor_tensor(c, a, y, ALU.mult).then_inc(self.s_chain, 1)
            dve.wait_ge(self.s_chain, 3 * i + 4)
            dve.scalar_tensor_tensor(out=y, in0=c, scalar=1.5, in1=y, op0=ALU.add, op1=ALU.mult).then_inc(self.s_chain, 1)
        dve.wait_ge(self.s_chain, self.CHAIN)

    def whole(self, dve):
        for t in range(TILES):
            self.stats(dve, t)
        self.rest(dve)


def setup(pr):
    nc = pr.nc
    s_w, s_zero, s_made, s_turned = pr.sems("setup", "w", "zero", "made", "turned")
    with ExitStack() as ctx:
        bias_rows = pr.sb(ctx)("bias_rows", [4 * KD, P], F32)
        bias_cols = pr.ps(ctx)("bias_cols", [P, 4 * KD], F32)
        block = ctx.enter_context(nc.Block())

        @block.tensor
        def _(pe):
            pe.wait_ge(s_w, 5 * 16)
            pe.wait_ge(s_made, 3)
            pe.transpose(bias_cols[:], bias_rows[:], pr.ident[0:4 * KD, 0:4 * KD]).then_inc(s_turned, 1)

        @block.vector
        def _(dve):
            dve.wait_ge(s_turned, 1)
            dve.tensor_copy(pr.bias_b[:].rearrange("p i k -> p (i k)"), bias_cols[:])

        @block.sync
        def _(sp):
            for b in range(NB):
                for c in range(CHUNKS):
                    sp.dma_start(pr.x[:, b * TILES + c * TPC:b * TILES + (c + 1) * TPC, :],
                                 pr.x_d[b, c * CHUNK:(c + 1) * CHUNK, :].rearrange("(t p) d -> p t d", p=P)).then_inc(pr.s_x[b], 16)

        @block.scalar
        def _(act):
            act.dma_start(pr.wr[:], pr.Wr.rearrange("(k p) e -> p k e", p=P)).then_inc(s_w, 16)
            for i, v in enumerate((pr.bq, pr.bk, pr.bv, pr.bo)):
                act.dma_start(bias_rows[KD * i:KD * i + KD, :], v.rearrange("(k p) -> k p", p=P)).then_inc(s_w, 16)

        @block.gpsimd
        def _(pool):
            pool.memset(pr.ident[:], 0.0).then_inc(s_zero, 1)
            pool.memset(pr.ident16[:], 0.0).then_inc(s_zero, 1)
            pool.memset(pr.ones[:], 1.0).then_inc(s_made, 1)
            pool.wait_ge(s_zero, 2)
            for m in (pr.ident, pr.ident16):
                pool.affine_select(out=m[:], in_=m[:], compare_op=ALU.not_equal, fill=1.0, base=0,
                                   pattern=[[-1, P]], channel_multiplier=1).then_inc(s_made, 1)


def head_attention(pr):
    nc, x = pr.nc, pr.x
    GH = 4
    GD = GH * HD
    NG = NB * GROUPS
    with ExitStack() as ctx:
        sb, ps = pr.sb(ctx), pr.ps(ctx)
        values = sb("a_values", [P, 2, TILES, GH, 32], F32)
        moving = sb("a_moving", [P, 2, GH // 2, S], F16)
        fixed = sb("a_fixed", [P, 2, GH, S], F16)
        split_m = sb("a_split_m", [P, 2, TPC, GH, 2, 2, HD], F16)
        split_f = sb("a_split_f", [P, 2, TPC, GH, 2, 2, HD], F16)
        UR, SR = 6, 3
        probs = sb("a_probs", [P, UR, 2, CHUNK], F32)
        osb = sb("a_osb", [P, 2, CHUNK], F32)
        rden = sb("a_rden", [P, TPC, GH], F32)
        onorm = sb("a_onorm", [P, TPC, GH, HD], F32)
        scores = ps("a_scores", [P, 2 * SR, CHUNK], F32)
        heads_out = ps("a_out", [P, CHUNK], F32)
        tbank = ps("a_tbank", [P, CHUNK], F32)
        turned = tbank[:].bitcast(F16)

        first_norm = Norm(pr, "a", 0)
        second_norm = Norm(pr, "a2", 1)
        next_norm = Norm(pr, "a3", 0)
        (s_zero, s_ones, s_xn, s_hi, s_lo_m, s_lo_f, s_tmov, s_tfix, s_emov, s_efix, s_scores, s_exp, s_mask, s_pv, s_ocopy,
         s_oturn, s_rden, s_onorm, s_added) = pr.sems(
            "a", "zero", "ones", "xn", "hi", "lo_m", "lo_f", "tmov", "tfix", "emov", "efix", "scores", "exp", "mask", "pv",
            "ocopy", "oturn", "rden", "onorm", "added")

        steps = [(G, c, kt) for G in range(NG) for c in range(CHUNKS) for kt in range(TPC * (c + 1))]
        outputs = [(G, c) for G in range(NG) for c in range(CHUNKS)]
        output_end, end = [], 0
        for G, c in outputs:
            end += TPC * (c + 1)
            output_end.append(end)
        GS = len(steps) // NG
        masked = [u for n, (G, c, kt) in enumerate(steps) if kt >= TPC * c for u in (2 * n, 2 * n + 1)]
        masks_by = [sum(1 for u in masked if u <= 2 * n + 1) for n in range(len(steps))]
        TURN_AT = {17: (0, 0), 19: (0, 1), 21: (1, 0), 23: (1, 1), 29: (2, 0), 31: (2, 1), 33: (3, 0), 35: (3, 1)}
        FIRST_TURN_AT = {0: (2, 0), 1: (2, 1), 2: (3, 0), 3: (3, 1)}

        def span(c, kt):
            skip = max(0, kt - TPC * c) * P
            return skip, CHUNK - skip

        with nc.Block() as block:
            @block.vector
            def _(dve):
                dve.memset(fixed[:].bitcast(F32), 0.0).then_inc(s_zero, 1)
                dve.wait_ge(pr.s_x[0], 16 * CHUNKS)
                first_norm.whole(dve)

                def split(job):
                    G, cc = divmod(job, CHUNKS)
                    b, g = divmod(G, GROUPS)
                    if cc == 0 and G >= 2:
                        dve.wait_ge(s_pv, output_end[CHUNKS * (G - 1) - 1])
                    for t in range(TPC * cc, TPC * (cc + 1)):
                        dve.tensor_scalar(values[:, G % 2, t, :, 0:HD],
                                          x[:, b * TILES + t, GD * g:GD * (g + 1)].rearrange("p (h e) -> p h e", h=GH),
                                          pr.mv[:, b, t, 0:1], pr.rstd[:, b, t:t + 1], ALU.subtract, ALU.mult).then_inc(s_xn, 1)
                    if job >= 2:
                        dve.wait_ge(s_tmov, job - 1)
                        dve.wait_ge(s_tfix, job - 1)
                    dve.wait_ge(s_xn, TPC * (job + 1))
                    v = values[:, G % 2, TPC * cc:TPC * (cc + 1), :, 0:HD].rearrange("p t h e -> p (t h) e")
                    twice = v.unsqueeze(2).to_broadcast([P, TPC * GH, 2, HD])
                    m = split_m[:, job % 2].rearrange("p t h i j e -> p (t h) i j e")
                    f = split_f[:, job % 2].rearrange("p t h i j e -> p (t h) i j e")
                    dve.tensor_copy(f[:, :, 0, :, :], twice).then_inc(s_hi, 1)
                    dve.tensor_copy(m[:, :, :, 0, :], twice).then_inc(s_hi, 1)
                    dve.wait_ge(s_hi, 2 * job + 2)
                    dve.tensor_tensor(m[:, :, :, 1, :], twice, m[:, :, :, 0, :], ALU.subtract).then_inc(s_lo_m, 1)

                def place(job):
                    G, cc = divmod(job, CHUNKS)
                    cut = slice(cc * CHUNK, (cc + 1) * CHUNK)
                    dve.wait_ge(s_tmov, job + 1)
                    dve.tensor_copy(moving[:, G % 2, :, cut], turned.rearrange("p (r n) -> p r n", r=GH // 2)).then_inc(s_emov, 1)
                    dve.wait_ge(s_tfix, job + 1)
                    if job == 0:
                        dve.wait_ge(s_zero, 1)
                    view = fixed[:, G % 2, :, cut].rearrange("p (r a) n -> p r a n", a=2)
                    src = turned.rearrange("p (r n) -> p r n", r=GH // 2)
                    dve.tensor_copy(view[0:64, :, 0, :], src[0:64]).then_inc(s_efix, 1)
                    dve.tensor_copy(view[64:128, :, 1, :], src[64:128]).then_inc(s_efix, 1)

                split(0)
                split(1)
                place(0)
                split(2)
                place(1)
                split(3)
                place(2)
                place(3)
                for i, (G, c) in enumerate(outputs):
                    b, g = divmod(G, GROUPS)
                    if G + 1 < NG and c >= 2:
                        for cc in (2 * (c - 2), 2 * (c - 2) + 1):
                            split(CHUNKS * (G + 1) + cc)
                            place(CHUNKS * (G + 1) + cc)
                    if i == CHUNKS + 1:
                        dve.wait_ge(pr.s_x[1], 16 * CHUNKS)
                        second_norm.whole(dve)
                    dve.wait_ge(s_pv, output_end[i])
                    dve.tensor_copy(osb[:, i % 2, :], heads_out[:]).then_inc(s_ocopy, 1)
                    dve.wait_ge(s_oturn, i + 1)
                    o = tbank[:].rearrange("p (t j e) -> p t j e", t=TPC, j=GH)
                    dve.reciprocal(rden[:], o[:, :, :, HD]).then_inc(s_rden, 1)
                    dve.wait_ge(s_rden, i + 1)
                    dve.tensor_tensor(onorm[:], o[:, :, :, 0:HD], rden[:].unsqueeze(3).to_broadcast([P, TPC, GH, HD]),
                                      ALU.mult).then_inc(s_onorm, 1)
                    dve.wait_ge(s_onorm, i + 1)
                    xv = x[:, b * TILES + c * TPC:b * TILES + (c + 1) * TPC, GD * g:GD * (g + 1)]\
                        .rearrange("p t (j e) -> p t j e", j=GH)
                    dve.tensor_tensor(xv, xv, onorm[:], ALU.add).then_inc(s_added, 1)
                    if i == CHUNKS * (GROUPS + 1) + 1:
                        dve.wait_ge(s_added, CHUNKS * GROUPS)
                        next_norm.whole(dve)

            @block.scalar
            def _(act):
                for n, (G, c, kt) in enumerate(steps):
                    skip, w = span(c, kt)
                    for a in range(2):
                        u = 2 * n + a
                        act.wait_ge(s_scores, u + 1)
                        if u >= UR:
                            act.wait_ge(s_pv, (u - UR) // 2 + 1)
                        act.activation(probs[:, u % UR, :, 0:w], scores[:, 2 * (u % SR):2 * (u % SR) + 2, 0:w], ACT.Exp,
                                       scale=HD ** -0.5).then_inc(s_exp, 1)

            @block.gpsimd
            def _(pool):
                pool.memset(values[:, :, :, :, HD:32].rearrange("p s t h e -> p (s t h) e"), 1.0).then_inc(s_ones, 1)

                def split_low(job):
                    G, cc = divmod(job, CHUNKS)
                    pool.wait_ge(s_hi, 2 * job + 2)
                    v = values[:, G % 2, TPC * cc:TPC * (cc + 1), :, 0:HD].rearrange("p t h e -> p (t h) e")
                    f = split_f[:, job % 2].rearrange("p t h i j e -> p (t h) i j e")
                    pool.tensor_tensor(f[:, :, 1, :, :], v.unsqueeze(2).to_broadcast([P, TPC * GH, 2, HD]), f[:, :, 0, :, :],
                                       ALU.subtract).then_inc(s_lo_f, 1)

                for job in range(CHUNKS):
                    split_low(job)
                for n, (G, c, kt) in enumerate(steps):
                    if kt >= TPC * c:
                        for u in (2 * n, 2 * n + 1):
                            pool.wait_ge(s_exp, u + 1)
                            tri = probs[:, u % UR, :, 0:P]
                            pool.affine_select(out=tri, in_=tri, compare_op=ALU.is_ge, fill=0.0, base=0,
                                               pattern=[[0, 2], [1, P]], channel_multiplier=-1).then_inc(s_mask, 1)
                    if n % GS + 1 in TURN_AT and TURN_AT[n % GS + 1][1] == 0 and G + 1 < NG:
                        split_low(CHUNKS * (G + 1) + TURN_AT[n % GS + 1][0])

            @block.tensor
            def _(pe):
                turns = [0, 0]

                def tbank_free():
                    sides, outs = turns
                    if sides:
                        pe.wait_ge(s_emov, (sides + 1) // 2)
                        pe.wait_ge(s_efix, 2 * (sides // 2))
                    if outs:
                        pe.wait_ge(s_added, outs)

                def turn(job, side):
                    tbank_free()
                    if side == 0:
                        pe.wait_ge(s_lo_m, job + 1)
                    else:
                        pe.wait_ge(s_lo_f, job + 1)
                    split, turned_job = ((split_m, s_tmov), (split_f, s_tfix))[side]
                    for t in range(TPC):
                        for r in range(GH // 2):
                            mm = pe.transpose(turned[:, (r * TPC + t) * P:(r * TPC + t + 1) * P],
                                              split[:, job % 2, t, 2 * r:2 * r + 2].rearrange("p a i j e -> p (a i j e)"),
                                              pr.ident16[:])
                    mm.then_inc(turned_job, 1)
                    turns[0] += 1

                def turn_out(i):
                    tbank_free()
                    pe.wait_ge(s_ocopy, i + 1)
                    for t in range(TPC):
                        mm = pe.transpose(tbank[:, t * P:(t + 1) * P], osb[:, i % 2, t * P:(t + 1) * P], pr.ident[:])
                    mm.then_inc(s_oturn, 1)
                    turns[1] += 1

                def products(n):
                    G, c, kt = steps[n]
                    i = CHUNKS * G + c
                    skip, w = span(c, kt)
                    if kt == 0 and i >= 1:
                        pe.wait_ge(s_ocopy, i)
                    pe.wait_ge(s_exp, 2 * n + 2)
                    pe.wait_ge(s_mask, masks_by[n])
                    for j in range(GH):
                        mm = pe.matmul(heads_out[32 * j:32 * j + 32, skip:CHUNK], values[:, G % 2, kt, j, :],
                                       probs[:, (2 * n + j // 2) % UR, j % 2, 0:w], start=(kt == 0),
                                       stop=(kt == TPC * (c + 1) - 1), skip_group_check=True)
                    mm.then_inc(s_pv, 1)

                for job in range(2):
                    for side in range(2):
                        turn(job, side)
                pe.wait_ge(s_ones, 1)
                turned_outputs = 0
                for n, (G, c, kt) in enumerate(steps):
                    skip, w = span(c, kt)
                    q0 = c * CHUNK + skip
                    if kt == 0:
                        pe.wait_ge(s_emov, CHUNKS * G + c + 1)
                        pe.wait_ge(s_efix, 2 * (CHUNKS * G + c + 1))
                    for a in range(2):
                        u = 2 * n + a
                        if u >= SR:
                            pe.wait_ge(s_exp, u - SR + 1)
                        for h in range(2):
                            mm = pe.matmul(scores[:, 2 * (u % SR) + h, 0:w], fixed[:, G % 2, 2 * a + h, kt * P:(kt + 1) * P],
                                           moving[:, G % 2, a, q0:q0 + w], start=True, stop=True)
                        mm.then_inc(s_scores, 1)
                    if n >= 1:
                        products(n - 1)
                    if turned_outputs < len(outputs) and n == output_end[turned_outputs] + 2:
                        turn_out(turned_outputs)
                        turned_outputs += 1
                    if G == 0 and n in FIRST_TURN_AT:
                        turn(*FIRST_TURN_AT[n])
                    if n % GS in TURN_AT and G + 1 < NG:
                        job, side = TURN_AT[n % GS]
                        turn(CHUNKS * (G + 1) + job, side)
                products(len(steps) - 1)
                for i in range(turned_outputs, len(outputs)):
                    turn_out(i)


class NormedColumns:

    RING = 4

    def __init__(self, pr, st, sb, banks):
        self.pr, self.banks = pr, banks
        self.xn = sb(f"{st}_xn", [P, self.RING, D], F32)
        self.hi = sb(f"{st}_xhi", [P, KD, S], F32R)
        self.lo = sb(f"{st}_xlo", [P, KD, S], F32R)
        self.s_xn, self.s_turn, self.s_hi, self.s_lo = pr.sems(st, "xn", "turn", "xhi", "xlo")

    def bank(self, use):
        return self.banks[use % len(self.banks)].rearrange("p (k n) -> p k n", k=KD)

    def norm(self, dve, use, b, pair):
        if use >= self.RING // 2:
            dve.wait_ge(self.s_turn, use - self.RING // 2 + 1)
        for i in range(2):
            t = 2 * pair + i
            dve.tensor_scalar(self.xn[:, (2 * use + i) % self.RING, :], self.pr.x[:, b * TILES + t, :],
                              self.pr.mv[:, b, t, 0:1], self.pr.rstd[:, b, t:t + 1], ALU.subtract, ALU.mult)\
               .then_inc(self.s_xn, 1)

    def turn(self, pe, use):
        n = len(self.banks)
        if use >= n:
            pe.wait_ge(self.s_lo, use - n + 1)
        pe.wait_ge(self.s_xn, 2 * use + 2)
        for i in range(2):
            for k in range(KD):
                mm = pe.transpose(self.bank(use)[:, k, i * P:(i + 1) * P],
                                  self.xn[:, (2 * use + i) % self.RING, k * P:(k + 1) * P], self.pr.ident[:])
        mm.then_inc(self.s_turn, 1)

    def high(self, act, use, pair):
        act.wait_ge(self.s_turn, use + 1)
        act.activation(self.hi[:, :, 2 * P * pair:2 * P * (pair + 1)], self.bank(use), ACT.Copy).then_inc(self.s_hi, 1)

    def low(self, dve, use, pair):
        dve.wait_ge(self.s_hi, use + 1)
        cols = slice(2 * P * pair, 2 * P * (pair + 1))
        dve.tensor_tensor(self.lo[:, :, cols], self.bank(use), self.hi[:, :, cols].bitcast(F32), ALU.subtract)\
           .then_inc(self.s_lo, 1)


def split_product(pe, out, fixed_hi, fixed_lo, moving_hi, moving_lo, first, last):
    pe.matmul(out, fixed_hi, moving_hi, start=first, stop=False)
    pe.matmul(out, fixed_hi, moving_lo, start=False, stop=False)
    return pe.matmul(out, fixed_lo, moving_hi, start=False, stop=last)


def add_columns(pr, st, turn_bank, b=0, scale=None):
    s_turned, s_added = pr.sems(st, "result_turned", "result_added")

    def tensor(pe, c, half, result, s_result):
        n = c * (TPC // 2) + half
        pe.wait_ge(s_result, KD * (c + 1))
        if n >= 1:
            pe.wait_ge(s_added, n)
        for t in range(2):
            for k in range(KD):
                q = (2 * half + t) * P
                mm = pe.transpose(turn_bank[:, (t * KD + k) * P:(t * KD + k + 1) * P], result[:, k, q:q + P], pr.ident[:])
        mm.then_inc(s_turned, 1)

    def vector(dve, c, half):
        n = c * (TPC // 2) + half
        dve.wait_ge(s_turned, n + 1)
        xv = pr.x[:, b * TILES + c * TPC + 2 * half:b * TILES + c * TPC + 2 * half + 2, :]
        turned = turn_bank[:].rearrange("p (t d) -> p t d", t=2)
        if scale is None:
            dve.tensor_tensor(xv, xv, turned, ALU.add).then_inc(s_added, 1)
        else:
            for t in range(2):
                add = dve.scalar_tensor_tensor(out=xv[:, t], in0=turned[:, t], scalar=scale[:, c % 2, 2 * half + t:2 * half + t + 1],
                                               in1=xv[:, t], op0=ALU.mult, op1=ALU.add)
            add.then_inc(s_added, 1)

    return tensor, vector, s_turned, s_added


def mixture(pr, layer):
    nc = pr.nc
    st = f"f{layer}"
    with ExitStack() as ctx:
        sb, ps = pr.sb(ctx), pr.ps(ctx)
        raw1 = sb(f"{st}_raw1", [P, TOPK, KD, F], F32)
        raw2 = sb(f"{st}_raw2", [P, TOPK, FT, D], F32)
        w1h = sb(f"{st}_w1h", [P, TOPK, KD, F], F32R)
        w1l = sb(f"{st}_w1l", [P, TOPK, KD, F], F32R)
        w2h = sb(f"{st}_w2h", [P, TOPK, FT, D], F32R)
        w2l = sb(f"{st}_w2l", [P, TOPK, FT, D], F32R)
        HR, LAG = 4, 3
        gel = sb(f"{st}_gelu", [P, HR, CHUNK], F32)
        hh = sb(f"{st}_hh", [P, HR, CHUNK], F32R)
        hl = sb(f"{st}_hl", [P, HR, CHUNK], F32R)
        ysb = sb(f"{st}_y", [P, KD, CHUNK], F32)
        xp = sb(f"{st}_xp", [P, 4, D], F32)
        BR = TOPK * (FT + KD)
        brow = sb(f"{st}_brow", [BR, P], F32)
        bcol = sb(f"{st}_bcol", [P, NB, BR], F32)
        b2w = sb(f"{st}_b2w", [P, NB, 2, KD], F32)
        pooled = sb(f"{st}_pooled", [P, KD], F32)
        logits = sb(f"{st}_logits", [1, E], F32)
        best = sb(f"{st}_best", [1, 8], F32)
        best_i = sb(f"{st}_best_i", [1, NB, 8], U32)
        gate = sb(f"{st}_gate", [1, 8], F32)
        gates = sb(f"{st}_gates", [P, NB, TOPK], F32)
        hps = ps(f"{st}_h", [P, 2, CHUNK], F32)
        yps = ps(f"{st}_ypsum", [P, 2 * KD, CHUNK], F32)
        misc = ps(f"{st}_misc", [P, CHUNK], F32)
        side = ps(f"{st}_side", [P, CHUNK], F32)
        cols = NormedColumns(pr, st, sb, [side[:]])
        norms = {b: Norm(pr, st, b) for b in range(NB)}

        (s_xp, s_sum, s_pooled, s_logit, s_logits, s_best, s_besti, s_diff, s_tanh, s_gate, s_spread, s_gates,
         s_b2w, s_bturn, s_bcol) = pr.sems(
            st, "xp", "sum", "pooled", "logit", "logits", "best", "besti", "diff", "tanh", "gate", "spread", "gates",
            "b2w", "bturn", "bcol")
        s_braw, s_wh, s_wl, s_h, s_gelu, s_hh, s_hl, s_used, s_y = pr.sems(
            st, "braw", "wh", "wl", "h", "gelu", "hh", "hl", "used", "y")
        s_raw = pr.sems(st, "raw1_0", "raw2_0", "raw1_1", "raw2_1")
        add_tensor, add_vector, s_rturned, s_added = add_columns(pr, st, misc)

        CS = TOPK * FT
        BS = CHUNKS * CS
        steps = [(q, c, e, j) for q in range(NB) for c in range(CHUNKS) for e in range(TOPK) for j in range(FT)]
        WP = 16

        def part(i):
            e, w, k = i // 8, (i % 8) // 4, i % 4
            if w == 0:
                views = [m[:, e, :, 256 * k:256 * k + 256] for m in (raw1, w1h, w1l)]
            else:
                views = [m[:, e, 2 * k:2 * k + 2, :] for m in (raw2, w2h, w2l)]
            return s_raw[2 * e + w], views

        sums = (29, 30, 31, 32, 33, 34)

        def beside(n):
            q, at = divmod(n, BS)
            work = []
            c, a = divmod(at, CS)
            last_batch = q == NB - 1
            if not (last_batch and c == CHUNKS - 1):
                first = {7: 0, 10: 1}
                pair = lambda i: (q, 2 * (c + 1) + i) if c < CHUNKS - 1 else (q + 1, i)
                for f, i in first.items():
                    if f <= a <= f + 2:
                        work.append((("norm", "turn", "low")[a - f], pair(i)))
            if not last_batch:
                if at < 16:
                    work.append(("stats", (1, at)))
                if at == 16:
                    work.append(("norms", 1))
                if at in sums:
                    work += [("xp", (q + 1, t)) for t in range(3 * sums.index(at), min(3 * sums.index(at) + 3, TILES))]
                if at - 1 in sums:
                    work += [("sum", (q + 1, t)) for t in range(3 * sums.index(at - 1), min(3 * sums.index(at - 1) + 3, TILES))]
                work += [(kind, q + 1) for kind, when in
                         (("pool", 37), ("logits", 38), ("route", 39), ("gate", 44), ("spread", 45), ("gates", 46),
                          ("turn_biases", 47), ("biases", 48)) if at == when]
                if 56 <= at:
                    work.append(("weights", (q + 1, at - 56)))
            else:
                if at < 16:
                    work.append(("stats", (0, at)))
                if at == 16:
                    work.append(("norms", 0))
            if at < 8:
                work.append(("weights", (q, 8 + at)))
            return work

        before = []
        for t in range(TILES):
            before += [("xp", (0, t)), ("sum", (0, t))]
        before += [("pool", 0), ("logits", 0), ("route", 0), ("norm", (0, 0)), ("norm", (0, 1)), ("turn", (0, 0)),
                   ("low", (0, 0)), ("turn", (0, 1)), ("low", (0, 1)), ("gate", 0), ("spread", 0), ("gates", 0),
                   ("turn_biases", 0), ("biases", 0)]
        before += [("weights", (0, i)) for i in range(8)]

        with nc.Block() as block:
            @block.sync
            def _(sp):
                for q in range(NB):
                    sp.wait_ge(s_besti, q + 1)
                    for e in range(TOPK):
                        n = sp.value_load(best_i[0:1, q, e:e + 1], min_val=0, max_val=E - 1)
                        if q >= 1:
                            sp.wait_ge(s_wl, WP * (q - 1) + 8 * e + 4)
                        sp.dma_start(raw1[:, e], pr.W1[bass.ds(n, 1)].rearrange("o (k p) f -> p (o k) f", p=P)).then_inc(s_raw[2 * e], 16)
                        if q >= 1:
                            sp.wait_ge(s_bturn, q)
                        sp.dma_start(brow[FT * e:FT * e + FT, :], pr.b1[bass.ds(n, 1)].rearrange("o (j p) -> (o j) p", p=P)).then_inc(s_braw, 16)
                        o = TOPK * FT + KD * e
                        sp.dma_start(brow[o:o + KD, :], pr.b2[bass.ds(n, 1)].rearrange("o (k p) -> (o k) p", p=P)).then_inc(s_braw, 16)
                        if q >= 1:
                            sp.wait_ge(s_wl, WP * (q - 1) + 8 * e + 8)
                        sp.dma_start(raw2[:, e], pr.W2[bass.ds(n, 1)].rearrange("o (j p) d -> p (o j) d", p=P)).then_inc(s_raw[2 * e + 1], 16)

            @block.tensor
            def _(pe):
                use = [0]
                routed, turned = [0], [0]

                def do(kind, what):
                    if kind == "turn":
                        pe.wait_ge(s_logits, routed[0])
                        if turned[0]:
                            pe.wait_ge(s_bcol, turned[0])
                        cols.turn(pe, use[0])
                        use[0] += 1
                    elif kind == "sum":
                        q, t = what
                        pe.wait_ge(s_xp, TILES * q + t + 1)
                        if t == 0 and q >= 1:
                            pe.wait_ge(cols.s_lo, use[0])
                        for k in range(KD):
                            mm = pe.matmul(side[:, k:k + 1], xp[:, t % 4, k * P:(k + 1) * P], pr.ones[:, 0:1],
                                           start=(t == 0 and k == 0), stop=(t == TILES - 1), skip_group_check=True)
                        mm.then_inc(s_sum, 1)
                    elif kind == "logits":
                        pe.wait_ge(s_pooled, what + 1)
                        for k in range(KD):
                            mm = pe.matmul(side[0:1, 0:E], pooled[:, k:k + 1], pr.wr[:, k, :], start=(k == 0), stop=(k == KD - 1))
                        mm.then_inc(s_logit, 1)
                        routed[0] += 1
                    elif kind == "spread":
                        pe.wait_ge(s_gate, what + 1)
                        pe.wait_ge(cols.s_lo, use[0])
                        pe.wait_ge(s_logits, what + 1)
                        pe.matmul(side[:, 0:TOPK], pr.ones[0:1, :], gate[0:1, 4:4 + TOPK], start=True, stop=True).then_inc(s_spread, 1)
                    elif kind == "turn_biases":
                        pe.wait_ge(s_braw, 4 * 16 * (what + 1))
                        pe.wait_ge(s_gates, what + 1)
                        pe.transpose(side[:, 0:BR], brow[:], pr.ident[0:BR, 0:BR]).then_inc(s_bturn, 1)
                        turned[0] += 1

                def up(n):
                    q, c, e, j = steps[n]
                    if c == 0:
                        pe.wait_ge(s_wl, WP * q + 8 * e + j // 2 + 1)
                    if e == 0 and j == 0:
                        pe.wait_ge(cols.s_lo, (TILES // 2) * q + 2 * (c + 1))
                    if n >= 2:
                        pe.wait_ge(s_gelu, n - 1)
                    for k in range(KD):
                        mm = split_product(pe, hps[:, n % 2, :], w1h[:, e, k, j * P:(j + 1) * P], w1l[:, e, k, j * P:(j + 1) * P],
                                           cols.hi[:, k, c * CHUNK:(c + 1) * CHUNK], cols.lo[:, k, c * CHUNK:(c + 1) * CHUNK],
                                           k == 0, k == KD - 1)
                    mm.then_inc(s_h, 1)

                def down(n):
                    q, c, e, j = steps[n]
                    chunk = CHUNKS * q + c
                    if c == 0:
                        pe.wait_ge(s_wl, WP * q + 8 * e + 4 + j // 2 + 1)
                    if e == 0 and j == 0 and chunk >= 2:
                        pe.wait_ge(s_y, KD * (chunk - 1))
                    pe.wait_ge(s_hl, n + 1)
                    for k in range(KD):
                        mm = split_product(pe, yps[:, KD * (chunk % 2) + k, :], w2h[:, e, j, k * P:(k + 1) * P],
                                           w2l[:, e, j, k * P:(k + 1) * P], hh[:, n % HR, :], hl[:, n % HR, :],
                                           e == 0 and j == 0, e == TOPK - 1 and j == FT - 1)
                    mm.then_inc(s_used, 1)

                for work in before:
                    do(*work)
                for n in range(len(steps) + LAG):
                    if n < len(steps):
                        up(n)
                    if n >= LAG:
                        down(n - LAG)
                    chunk, at = divmod(n, CS)
                    if 1 <= chunk < NB * CHUNKS and at in (4, 6):
                        add_tensor(pe, chunk - 1, (at - 4) // 2, ysb, s_y)
                    if n < len(steps):
                        for work in beside(n):
                            do(*work)
                for half in range(2):
                    add_tensor(pe, NB * CHUNKS - 1, half, ysb, s_y)

            @block.scalar
            def _(act):
                use = [0]

                def do(kind, what):
                    if kind == "turn":
                        cols.high(act, use[0], what[1])
                        use[0] += 1
                    elif kind == "route":
                        act.wait_ge(s_diff, what + 1)
                        act.activation(gate[0:1, 2:3], gate[0:1, 0:1], ACT.Tanh, scale=0.5).then_inc(s_tanh, 1)
                        act.activation(gate[0:1, 3:4], gate[0:1, 0:1], ACT.Tanh, scale=-0.5).then_inc(s_tanh, 1)
                    elif kind == "weights":
                        q, i = what
                        arrived, (raw, hi, lo) = part(i)
                        act.wait_ge(arrived, 16 * (q + 1))
                        if q >= 1:
                            last = (q - 1) * BS + (CHUNKS - 1) * CS + FT * (i // 8 + 1)
                            act.wait_ge(s_h if i % 8 < 4 else s_used, last)
                        act.activation(hi, raw, ACT.Copy).then_inc(s_wh, 1)

                for work in before:
                    do(*work)
                for n, (q, c, e, j) in enumerate(steps):
                    if c == 0 and e == 0 and j == 0:
                        act.wait_ge(s_bcol, q + 1)
                    act.wait_ge(s_h, n + 1)
                    if n >= HR:
                        act.wait_ge(s_hl, n - HR + 1)
                    act.activation(gel[:, n % HR, :], hps[:, n % 2, :], ACT.Gelu, bias=bcol[:, q, FT * e + j:FT * e + j + 1])\
                       .then_inc(s_gelu, 1)
                    for work in beside(n):
                        do(*work)

            @block.vector
            def _(dve):
                normed, lows = [0], [0]

                def do(kind, what):
                    if kind == "norm":
                        q, pair = what
                        cols.norm(dve, normed[0], q, pair)
                        normed[0] += 1
                    elif kind == "low":
                        q, pair = what
                        cols.low(dve, lows[0], pair)
                        lows[0] += 1
                    elif kind == "stats":
                        norms[what[0]].stats(dve, what[1])
                    elif kind == "norms":
                        norms[what].rest(dve)
                    elif kind == "xp":
                        q, t = what
                        n = TILES * q + t
                        if n >= 4:
                            dve.wait_ge(s_sum, n - 3)
                        dve.tensor_scalar(xp[:, t % 4, :], pr.x[:, q * TILES + t, :], pr.mv[:, q, t, 0:1],
                                          pr.rstd[:, q, t:t + 1], ALU.subtract, ALU.mult).then_inc(s_xp, 1)
                    elif kind == "pool":
                        q = what
                        dve.wait_ge(s_sum, TILES * (q + 1))
                        dve.tensor_scalar(pooled[:], side[:, 0:KD], 1.0 / S, None, ALU.mult).then_inc(s_pooled, 1)
                    elif kind == "route":
                        q = what
                        dve.wait_ge(s_logit, q + 1)
                        dve.tensor_copy(logits[:], side[0:1, 0:E]).then_inc(s_logits, 1)
                        dve.wait_ge(s_logits, q + 1)
                        dve.max(best[:], logits[:]).then_inc(s_best, 1)
                        dve.wait_ge(s_best, q + 1)
                        dve.max_index(best_i[:, q, :], best[:], logits[:]).then_inc(s_besti, 1)
                        dve.tensor_tensor(gate[0:1, 0:1], best[0:1, 0:1], best[0:1, 1:2], ALU.subtract).then_inc(s_diff, 1)
                    elif kind == "gate":
                        q = what
                        dve.wait_ge(s_tanh, 2 * (q + 1))
                        dve.tensor_scalar(gate[0:1, 4:6], gate[0:1, 2:4], 0.5, 0.5, ALU.mult, ALU.add).then_inc(s_gate, 1)
                    elif kind == "gates":
                        q = what
                        dve.wait_ge(s_spread, q + 1)
                        dve.tensor_copy(gates[:, q, :], side[:, 0:TOPK]).then_inc(s_gates, 1)
                    elif kind == "biases":
                        q = what
                        dve.wait_ge(s_bturn, q + 1)
                        dve.tensor_copy(bcol[:, q, :], side[:, 0:BR]).then_inc(s_bcol, 1)
                        dve.wait_ge(s_bcol, q + 1)
                        dve.wait_ge(s_gates, q + 1)
                        o = TOPK * FT
                        dve.tensor_scalar(b2w[:, q, 0, :], bcol[:, q, o:o + KD], gates[:, q, 0:1], None, ALU.mult).then_inc(s_b2w, 1)
                        dve.wait_ge(s_b2w, 2 * q + 1)
                        dve.scalar_tensor_tensor(out=b2w[:, q, 1, :], in0=bcol[:, q, o + KD:o + 2 * KD], scalar=gates[:, q, 1:2],
                                                 in1=b2w[:, q, 0, :], op0=ALU.mult, op1=ALU.add).then_inc(s_b2w, 1)
                    elif kind == "weights":
                        q, i = what
                        arrived, (raw, hi, lo) = part(i)
                        dve.wait_ge(s_wh, WP * q + i + 1)
                        dve.tensor_tensor(lo, raw, hi.bitcast(F32), ALU.subtract).then_inc(s_wl, 1)

                def result(chunk):
                    q = chunk // CHUNKS
                    dve.wait_ge(s_used, (chunk + 1) * CS)
                    dve.wait_ge(s_b2w, 2 * (q + 1))
                    if chunk >= 1:
                        dve.wait_ge(s_rturned, (TPC // 2) * chunk)
                    for k in range(KD):
                        dve.tensor_scalar(ysb[:, k, :], yps[:, KD * (chunk % 2) + k, :], b2w[:, q, 1, k:k + 1], None, ALU.add)\
                           .then_inc(s_y, 1)

                for work in before:
                    do(*work)
                for n, (q, c, e, j) in enumerate(steps):
                    dve.wait_ge(s_gelu, n + 1)
                    if n >= HR:
                        dve.wait_ge(s_used, n - HR + 1)
                    dve.tensor_scalar(hh[:, n % HR, :], gel[:, n % HR, :], gates[:, q, e:e + 1], None, ALU.mult).then_inc(s_hh, 1)
                    dve.wait_ge(s_hh, n + 1)
                    dve.scalar_tensor_tensor(out=hl[:, n % HR, :], in0=gel[:, n % HR, :], scalar=gates[:, q, e:e + 1],
                                             in1=hh[:, n % HR, :].bitcast(F32), op0=ALU.mult, op1=ALU.subtract).then_inc(s_hl, 1)
                    chunk, at = divmod(n, CS)
                    if chunk >= 1 and at == 3:
                        result(chunk - 1)
                    if chunk >= 1 and at in (5, 6):
                        add_vector(dve, chunk - 1, at - 5)
                    for work in beside(n):
                        do(*work)
                result(NB * CHUNKS - 1)
                for half in range(2):
                    add_vector(dve, NB * CHUNKS - 1, half)


class DistanceWeights:

    def __init__(self, pr, ctx):
        nc = pr.nc
        sb = pr.sb(ctx)
        self.hi, self.lo = {}, {}
        for name in ("q", "k", "vo"):
            self.hi[name] = sb(f"w{name}_hi", [P, KD, D], F32R)
            self.lo[name] = sb(f"w{name}_lo", [P, KD, D], F32R)
        s_w, s_vturn, s_vcol, s_vo, s_bvo, s_vo32, s_hi, s_lo, s_bias = pr.sems(
            "dw", "w", "vturn", "vcol", "vo", "bvo", "vo32", "hi", "lo", "bias")
        s_wide, s_bo = pr.sems("dw", "wide", "bo")
        with ExitStack() as tmp:
            tsb, ps = pr.sb(tmp), pr.ps(tmp)
            raw = {n: tsb(f"w{n}_raw", [P, KD, D], F32) for n in ("q", "k", "v", "o", "vo")}
            vcol = tsb("wv_turned", [P, KD, D], F32)
            turn = ps("dw_turn", [P, KD, D], F32)
            prod = ps("dw_prod", [P, KD, D], F32)
            bias = ps("dw_bias", [P, D], F32)
            bv_wide = tsb("bv_wide", [P, KD, P], F32)
            bo_row = tsb("bo_row", [1, D], F32)
            block = tmp.enter_context(nc.Block())

            @block.sync
            def _(sp):
                sp.dma_start(bo_row[:], pr.bo.rearrange("(o d) -> o d", o=1)).then_inc(s_bo, 16)
                for n, w in (("v", pr.Wv), ("o", pr.Wo), ("q", pr.Wq), ("k", pr.Wk)):
                    sp.dma_start(raw[n][:], w.rearrange("(k p) n -> p k n", p=P)).then_inc(s_w, 16)

            @block.tensor
            def _(pe):
                pe.wait_ge(s_w, 64)
                for r in range(KD):
                    for k in range(KD):
                        mm = pe.transpose(turn[:, k, r * P:(r + 1) * P], raw["v"][:, r, k * P:(k + 1) * P], pr.ident[:])
                mm.then_inc(s_vturn, 1)
                pe.wait_ge(s_vcol, 1)
                for r in range(KD):
                    for k in range(KD):
                        mm = pe.matmul(prod[:, r, :], vcol[:, k, r * P:(r + 1) * P], raw["o"][:, k, :],
                                       start=(k == 0), stop=(k == KD - 1))
                mm.then_inc(s_vo, 1)
                pe.wait_ge(s_wide, KD)
                pe.wait_ge(s_bo, 16)
                for k in range(KD):
                    pe.matmul(bias[:], bv_wide[:, k, :], raw["o"][:, k, :], start=(k == 0), stop=False)
                pe.matmul(bias[:], pr.ones[0:1, :], bo_row[:], start=False, stop=True).then_inc(s_bvo, 1)

            @block.vector
            def _(dve):
                for k in range(KD):
                    dve.tensor_scalar(bv_wide[:, k, :], pr.ones[:], pr.bias_b[:, 2, k:k + 1], None, ALU.mult).then_inc(s_wide, 1)
                dve.wait_ge(s_vturn, 1)
                dve.tensor_copy(vcol[:], turn[:]).then_inc(s_vcol, 1)
                dve.wait_ge(s_vo, 1)
                dve.tensor_copy(raw["vo"][:], prod[:]).then_inc(s_vo32, 1)
                dve.wait_ge(s_vo32, 1)
                dve.wait_ge(s_w, 64)
                for n in ("q", "k", "vo"):
                    dve.tensor_copy(self.hi[n][:], raw[n][:]).then_inc(s_hi, 1)
                for i, n in enumerate(("q", "k", "vo")):
                    dve.wait_ge(s_hi, i + 1)
                    dve.tensor_tensor(self.lo[n][:], raw[n][:], self.hi[n][:].bitcast(F32), ALU.subtract).then_inc(s_lo, 1)
                dve.wait_ge(s_bvo, 1)
                dve.tensor_copy(pr.bvo[:], bias[:]).then_inc(s_bias, 1)


def distance_weights(pr, ctx):
    return DistanceWeights(pr, ctx)


def distance_attention(pr, b, w):
    nc = pr.nc
    st = f"b{b}"
    with ExitStack() as ctx:
        sb, ps = pr.sb(ctx), pr.ps(ctx)
        hi = {n: sb(f"{st}_{n}hi", [P, KD, S], F32R) for n in "qk"}
        lo = {n: sb(f"{st}_{n}lo", [P, KD, S], F32R) for n in "qk"}
        vhi = sb(f"{st}_vhi", [P, TILES, D], F32R)
        vlo = sb(f"{st}_vlo", [P, TILES, D], F32R)
        qsq = sb(f"{st}_qsq", [P, S], F32)
        nksq = sb(f"{st}_nksq", [P, TILES], F32)
        banks = ps(f"{st}_banks", [P, 3, CHUNK], F32)
        outs = ps(f"{st}_outs", [P, 2 * KD, CHUNK], F32)
        misc = ps(f"{st}_misc", [P, CHUNK], F32)

        with ExitStack() as part:
            psb = pr.sb(part)
            cols = NormedColumns(pr, st, psb, [banks[:, i, :] for i in range(2)])
            vbank = banks[:, 2, :]
            qk32 = psb(f"{st}_qk32", [P, 2, KD, CHUNK], F32)
            square = psb(f"{st}_square", [P, 2, KD, CHUNK], F32)
            s_v, s_vhi, s_vlo, s_p, s_p32, s_phi, s_plo, s_sq, s_len, s_lenc = pr.sems(
                st, "v", "vhi", "vlo", "p", "p32", "phi", "plo", "sq", "len", "lenc")
            (s_xb,) = pr.sems(st, "xb")
            tasks = [(n, c) for c in range(CHUNKS) for n in "kq"]
            with nc.Block() as block:
                @block.tensor
                def _(pe):
                    def values(u):
                        pe.wait_ge(cols.s_lo, u + 1)
                        if u >= 1:
                            pe.wait_ge(s_vlo, u)
                        for t in (2 * u, 2 * u + 1):
                            for k in range(KD):
                                tok = slice(t * P, (t + 1) * P)
                                mm = split_product(pe, vbank[:, (t % 2) * D:(t % 2 + 1) * D], cols.hi[:, k, tok], cols.lo[:, k, tok],
                                                   w.hi["vo"][:, k, :], w.lo["vo"][:, k, :], k == 0, k == KD - 1)
                        mm.then_inc(s_v, 1)

                    def project(i):
                        n, c = tasks[i]
                        pe.wait_ge(cols.s_lo, 2 * (c + 1))
                        for m in range(KD):
                            j = KD * i + m
                            if j >= 4:
                                pe.wait_ge(s_p32, j - 3)
                            for k in range(KD):
                                mm = split_product(pe, outs[:, j % 4, :], w.hi[n][:, k, m * P:(m + 1) * P],
                                                   w.lo[n][:, k, m * P:(m + 1) * P], cols.hi[:, k, c * CHUNK:(c + 1) * CHUNK],
                                                   cols.lo[:, k, c * CHUNK:(c + 1) * CHUNK], k == 0, k == KD - 1)
                            mm.then_inc(s_p, 1)

                    def lengths(i):
                        n, c = tasks[i]
                        pe.wait_ge(s_sq, KD * (i + 1))
                        if i >= 1:
                            pe.wait_ge(s_lenc, i)
                        if n == "q":
                            for m in range(KD):
                                mm = pe.matmul(misc[:], pr.ones[:], square[:, i % 2, m, :], start=(m == 0), stop=(m == KD - 1))
                        else:
                            for t in range(TPC):
                                for m in range(KD):
                                    mm = pe.matmul(misc[:, t:t + 1], square[:, i % 2, m, t * P:(t + 1) * P], pr.ones[:, 0:1],
                                                   start=(m == 0), stop=(m == KD - 1))
                        mm.then_inc(s_len, 1)

                    cols.turn(pe, 0)
                    cols.turn(pe, 1)
                    for i in range(len(tasks)):
                        if i + 2 < len(tasks):
                            cols.turn(pe, i + 2)
                        values(i)
                        project(i)
                        if i >= 1:
                            lengths(i - 1)
                    lengths(len(tasks) - 1)

                @block.scalar
                def _(act):
                    cols.high(act, 0, 0)
                    cols.high(act, 1, 1)
                    for i, (n, c) in enumerate(tasks):
                        if i + 2 < len(tasks):
                            cols.high(act, i + 2, i + 2)
                        act.wait_ge(s_v, i + 1)
                        act.activation(vhi[:, 2 * i:2 * i + 2, :], vbank.rearrange("p (t d) -> p t d", t=2),
                                       ACT.Copy).then_inc(s_vhi, 1)
                        for m in range(KD):
                            j = KD * i + m
                            act.wait_ge(s_p, j + 1)
                            if i >= 2:
                                act.wait_ge(s_sq, j - 3)
                                act.wait_ge(s_plo, j - 3)
                            act.activation(qk32[:, i % 2, m, :], outs[:, j % 4, :], ACT.Identity,
                                           bias=pr.bias_b[:, 0 if n == "q" else 1, m:m + 1]).then_inc(s_p32, 1)

                @block.gpsimd
                def _(pool):
                    for i in range(len(tasks)):
                        for t in (2 * i, 2 * i + 1):
                            pool.wait_ge(cols.s_xn, t + 1)
                            xv = pr.x[:, b * TILES + t, :]
                            pool.tensor_tensor(xv, xv, pr.bvo[:], ALU.add).then_inc(s_xb, 1)
                        for m in range(KD):
                            pool.wait_ge(s_p32, KD * i + m + 1)
                            if i >= 2:
                                pool.wait_ge(s_len, i - 1)
                            t32 = qk32[:, i % 2, m, :]
                            pool.tensor_tensor(square[:, i % 2, m, :], t32, t32, ALU.mult).then_inc(s_sq, 1)

                @block.vector
                def _(dve):
                    def read_lengths(i):
                        n, c = tasks[i]
                        dve.wait_ge(s_len, i + 1)
                        if n == "q":
                            dve.tensor_copy(qsq[:, c * CHUNK:(c + 1) * CHUNK], misc[:]).then_inc(s_lenc, 1)
                        else:
                            dve.tensor_scalar(nksq[:, c * TPC:(c + 1) * TPC], misc[:, 0:TPC], -1.0, None, ALU.mult).then_inc(s_lenc, 1)

                    for u in range(2):
                        cols.norm(dve, u, b, u)
                    for u in range(2):
                        cols.low(dve, u, u)
                    cols.norm(dve, 2, b, 2)
                    for i, (n, c) in enumerate(tasks):
                        if i + 3 < len(tasks):
                            cols.norm(dve, i + 3, b, i + 3)
                        if i + 2 < len(tasks):
                            cols.low(dve, i + 2, i + 2)
                        dve.wait_ge(s_vhi, i + 1)
                        dve.tensor_tensor(vlo[:, 2 * i:2 * i + 2, :], vbank.rearrange("p (t d) -> p t d", t=2),
                                          vhi[:, 2 * i:2 * i + 2, :].bitcast(F32), ALU.subtract).then_inc(s_vlo, 1)
                        for m in range(KD):
                            j = KD * i + m
                            dve.wait_ge(s_p32, j + 1)
                            cut = slice(c * CHUNK, (c + 1) * CHUNK)
                            dve.tensor_copy(hi[n][:, m, cut], qk32[:, i % 2, m, :]).then_inc(s_phi, 1)
                            dve.wait_ge(s_phi, j + 1)
                            dve.tensor_tensor(lo[n][:, m, cut], qk32[:, i % 2, m, :], hi[n][:, m, cut].bitcast(F32),
                                              ALU.subtract).then_inc(s_plo, 1)
                        if i >= 1:
                            read_lengths(i - 1)
                    read_lengths(len(tasks) - 1)

        with ExitStack() as part:
            psb = pr.sb(part)
            R = 4
            dist = psb(f"{st}_dist", [P, R, CHUNK], F32)
            score = psb(f"{st}_score", [P, R, CHUNK], F32)
            p32 = psb(f"{st}_p32", [P, R, CHUNK], F32)
            phi = psb(f"{st}_phi", [P, R, CHUNK], F32R)
            plo = psb(f"{st}_plo", [P, R, CHUNK], F32R)
            psum_acc = psb(f"{st}_psum_acc", [P, 2, CHUNK], F32)
            rden = psb(f"{st}_rden", [P, 2, TPC], F32)
            ysb = psb(f"{st}_y", [P, KD, CHUNK], F32)
            s_qk, s_dist, s_score, s_p32, s_phi, s_plo, s_acc, s_pv, s_den, s_rden, s_y = pr.sems(
                st, "qk", "dist", "score", "prob", "probhi", "problo", "acc", "pv", "den", "rden", "y")
            add_tensor, add_vector, s_rturned, s_added = add_columns(pr, st, misc, b, rden)
            next_norm = Norm(pr, st, 1 - b)
            steps = [(c, kt) for c in range(CHUNKS) for kt in range(TILES)]

            def summed(n):
                return (TILES - 1) * (n // TILES) + max(n % TILES, 1)

            with nc.Block() as block:
                @block.tensor
                def _(pe):
                    def scores(n):
                        c, kt = steps[n]
                        if n >= 3:
                            pe.wait_ge(s_dist, n - 2)
                        for k in range(KD):
                            mm = split_product(pe, banks[:, n % 3, :], hi["k"][:, k, kt * P:(kt + 1) * P],
                                               lo["k"][:, k, kt * P:(kt + 1) * P], hi["q"][:, k, c * CHUNK:(c + 1) * CHUNK],
                                               lo["q"][:, k, c * CHUNK:(c + 1) * CHUNK], k == 0, k == KD - 1)
                        mm.then_inc(s_qk, 1)

                    def values(n):
                        c, kt = steps[n]
                        if kt == 0 and c >= 2:
                            pe.wait_ge(s_y, KD * (c - 1))
                        pe.wait_ge(s_phi, n + 1)
                        pe.wait_ge(s_plo, n + 1)
                        for m in range(KD):
                            mm = split_product(pe, outs[:, KD * (c % 2) + m, :], vhi[:, kt, m * P:(m + 1) * P],
                                               vlo[:, kt, m * P:(m + 1) * P], phi[:, n % R, :], plo[:, n % R, :],
                                               kt == 0, kt == TILES - 1)
                        mm.then_inc(s_pv, 1)

                    def denominator(c):
                        pe.wait_ge(s_acc, (TILES - 1) * (c + 1))
                        if c >= 1:
                            pe.wait_ge(s_added, (TPC // 2) * c)
                        for t in range(TPC):
                            mm = pe.matmul(misc[:, t:t + 1], psum_acc[:, c % 2, t * P:(t + 1) * P], pr.ones[:, 0:1],
                                           start=True, stop=True)
                        mm.then_inc(s_den, 1)

                    LAG = 3
                    for n in range(len(steps) + LAG):
                        if n < len(steps):
                            scores(n)
                        if n >= LAG:
                            values(n - LAG)
                        c, at = divmod(n, TILES)
                        if 1 <= c < CHUNKS and at == 3:
                            denominator(c - 1)
                        if 1 <= c < CHUNKS and at == 7:
                            pe.wait_ge(s_rden, c)
                        if 1 <= c < CHUNKS and at in (7, 9):
                            add_tensor(pe, c - 1, (at - 7) // 2, ysb, s_y)
                    denominator(CHUNKS - 1)
                    pe.wait_ge(s_rden, CHUNKS)
                    for half in range(2):
                        add_tensor(pe, CHUNKS - 1, half, ysb, s_y)

                @block.scalar
                def _(act):
                    def second(n):
                        act.wait_ge(s_score, n + 1)
                        if n >= R:
                            act.wait_ge(s_plo, n - R + 1)
                            act.wait_ge(s_acc, summed(n - R))
                        act.activation(p32[:, n % R, :], score[:, n % R, :], ACT.Exp).then_inc(s_p32, 1)
                    def result(c):
                        act.wait_ge(s_pv, TILES * (c + 1))
                        if c >= 1:
                            act.wait_ge(s_rturned, (TPC // 2) * c)
                        for m in range(KD):
                            act.activation(ysb[:, m, :], outs[:, KD * (c % 2) + m, :], ACT.Copy).then_inc(s_y, 1)

                    for n, (c, kt) in enumerate(steps):
                        act.wait_ge(s_dist, n + 1)
                        if n >= R:
                            act.wait_ge(s_p32, n - R + 1)
                        act.activation(score[:, n % R, :], dist[:, n % R, :], ACT.Exp, scale=-1.0,
                                       bias=nksq[:, kt:kt + 1]).then_inc(s_score, 1)
                        if n >= 1:
                            second(n - 1)
                        if c >= 1 and kt == 4:
                            result(c - 1)
                    second(len(steps) - 1)
                    result(CHUNKS - 1)

                @block.gpsimd
                def _(pool):
                    done = 0
                    for n, (c, kt) in enumerate(steps):
                        if kt == 0:
                            continue
                        pool.wait_ge(s_p32, n + 1)
                        acc = psum_acc[:, c % 2, :]
                        if kt == 1:
                            if c >= 2:
                                pool.wait_ge(s_den, c - 1)
                            pool.tensor_tensor(acc, p32[:, (n - 1) % R, :], p32[:, n % R, :], ALU.add).then_inc(s_acc, 1)
                        else:
                            pool.wait_ge(s_acc, done)
                            pool.tensor_tensor(acc, acc, p32[:, n % R, :], ALU.add).then_inc(s_acc, 1)
                        done += 1

                @block.vector
                def _(dve):
                    def halves(n):
                        dve.wait_ge(s_p32, n + 1)
                        if n >= R:
                            dve.wait_ge(s_pv, n - R + 1)
                        dve.tensor_copy(phi[:, n % R, :], p32[:, n % R, :]).then_inc(s_phi, 1)
                        dve.wait_ge(s_phi, n + 1)
                        dve.tensor_tensor(plo[:, n % R, :], p32[:, n % R, :], phi[:, n % R, :].bitcast(F32), ALU.subtract)\
                           .then_inc(s_plo, 1)

                    def denominators(c):
                        dve.wait_ge(s_den, c + 1)
                        dve.reciprocal(rden[:, c % 2, :], misc[:, 0:TPC]).then_inc(s_rden, 1)

                    for n in range(len(steps) + 2):
                        if n < len(steps):
                            c, kt = steps[n]
                            dve.wait_ge(s_qk, n + 1)
                            if n >= R:
                                dve.wait_ge(s_score, n - R + 1)
                            dve.scalar_tensor_tensor(out=dist[:, n % R, :], in0=banks[:, n % 3, :], scalar=-2.0,
                                                     in1=qsq[:, c * CHUNK:(c + 1) * CHUNK], op0=ALU.mult, op1=ALU.add)\
                               .then_inc(s_dist, 1)
                        if n >= 2:
                            halves(n - 2)
                        c, at = divmod(n, TILES)
                        if 8 <= n < 8 + TILES:
                            next_norm.stats(dve, n - 8)
                        if n == 8 + TILES:
                            next_norm.rest(dve)
                        if 1 <= c < CHUNKS and at == 4:
                            denominators(c - 1)
                        if 1 <= c < CHUNKS and at in (7, 9):
                            add_vector(dve, c - 1, (at - 7) // 2)
                    denominators(CHUNKS - 1)
                    for half in range(2):
                        add_vector(dve, CHUNKS - 1, half)


def finish(pr):
    s_out = pr.s_out
    with pr.nc.Block() as block:
        @block.sync
        def _(sp):
            for b in range(NB):
                sp.dma_start(pr.out_d[b].rearrange("(t p) d -> p t d", p=P), pr.x[:, b * TILES:(b + 1) * TILES, :]).then_inc(s_out, 16)
            sp.wait_ge(s_out, 32)


def hybrid_block(nc, *args):
    with ExitStack() as ctx:
        pr = Program(nc, ctx, args)
        setup(pr)
        head_attention(pr)
        pr.end_stage()
        mixture(pr, 0)
        pr.end_stage()
        with ExitStack() as weights_ctx:
            w = DistanceWeights(pr, weights_ctx)
            for b in range(NB):
                distance_attention(pr, b, w)
                pr.end_stage()
        mixture(pr, 1)
        pr.end_stage()
        finish(pr)


_INS = ["L0_attn_a_x", "L0_attn_b_Wq", "L0_attn_b_bq", "L0_attn_b_Wk", "L0_attn_b_bk", "L0_attn_b_Wv",
        "L0_attn_b_bv", "L0_attn_b_Wo", "L0_attn_b_bo", "L0_ffn_Wr", "L0_ffn_W1", "L0_ffn_b1", "L0_ffn_W2", "L0_ffn_b2"]


def kernel(**inputs):
    import concourse.bacc as _bacc
    from concourse.bass_utils import run_bass_kernel_spmd as _run

    nc = _bacc.Bacc("TRN2", target_bir_lowering=False, num_devices=1)
    arrays, args = {}, []
    for name in _INS:
        a = np.ascontiguousarray(inputs[name])
        arrays[f"in_{name}"] = a
        args.append(nc.dram_tensor(f"in_{name}", a.shape, mybir.dt.from_np(a.dtype), kind="ExternalInput").ap())
    args.append(nc.dram_tensor("out_0", (NB, S, D), F32, kind="ExternalOutput").ap())
    hybrid_block(nc, *args)
    r = _run(nc, [arrays], core_ids=[0])
    return r.results[0]["out_0"]
```

```python
from contextlib import ExitStack

import numpy as np

import concourse.bass as bass
from concourse import mybir

F32 = mybir.dt.float32
F32R = mybir.dt.float32r
F16 = mybir.dt.float16
U32 = mybir.dt.uint32
I32 = mybir.dt.int32
ALU = mybir.AluOpType
ACT = mybir.ActivationFunctionType
AX = mybir.AxisListType

P = 128
EPS = 1e-5
NB, S, D = 2, 2048, 256
TILES = S // P
CHUNK = 512
CHUNKS = S // CHUNK
TPC = CHUNK // P
KD = D // P
HEADS, HD = 16, 16
PAIRS = HEADS // 2
GROUPS = HEADS // 4
E, F = 8, 1024
FT = F // P
TOPK = 2


class Program:

    def __init__(self, nc, ctx, args):
        self.nc, self.stage_sems = nc, []
        self.s_out = nc.alloc_semaphore(name="out_stored")
        self.s_x = [[nc.alloc_semaphore(name=f"x_loaded{b}_{c}") for c in range(CHUNKS)] for b in range(NB)]
        self.s_wr = nc.alloc_semaphore(name="router_loaded")
        self.s_dw = nc.alloc_semaphore(name="distance_weights_loaded")
        self.s_db = nc.alloc_semaphore(name="distance_biases_loaded")
        (self.x_d, self.Wq, self.bq, self.Wk, self.bk, self.Wv, self.bv, self.Wo, self.bo,
         self.Wr, self.W1, self.b1, self.W2, self.b2, self.out_d) = args
        sb = self.sb(ctx)
        self.x = sb("x", [P, NB * TILES, D], F32)
        self.ident = sb("ident", [P, P], F32)
        self.ident16 = sb("ident16", [P, P], F16)
        self.ones = sb("ones", [P, P], F32)
        self.wr = sb("wr", [P, KD, E], F32)
        self.stats = sb("stats", [P, TILES, 6], F32)
        self.mv = sb("mv", [P, NB, TILES, 2], F32)
        self.rstd = sb("rstd", [P, NB, TILES], F32)
        self.vare = sb("vare", [P, TILES], F32)
        self.newton = sb("newton", [P, 2, TILES], F32)
        self.shift = sb("shift", [P, TILES], F32)
        self.shift_sum = sb("shift_sum", [P, 1], F32)
        self.gathered = sb("gathered", [P, D], F32)
        self.pooled = sb("pooled", [P, KD], F32)
        self.logits = sb("logits", [1, E], F32)
        self.best = sb("best", [1, 8], F32)
        self.best_i = sb("best_i", [1, NB, 8], U32)
        self.lead = sb("lead", [1, NB], F32)
        self.bias_b = sb("bias_b", [P, 3, KD], F32)
        self.bvo = sb("bvo", [P, D], F32)

    def sb(self, ctx):
        return lambda name, shape, dt: ctx.enter_context(self.nc.sbuf_tensor(name, shape, dt))

    def ps(self, ctx):
        return lambda name, shape, dt: ctx.enter_context(self.nc.psum_tensor(name, shape, dt))

    def sems(self, stage, *names):
        made = [self.nc.alloc_semaphore(name=f"{stage}_{n}") for n in names]
        self.stage_sems += made
        return made

    def end_stage(self):
        self.nc.clear_and_free_semaphores(self.stage_sems)
        self.nc.all_engine_barrier()
        self.stage_sems = []


class DistanceInputs:

    def __init__(self, pr, ctx):
        sb = pr.sb(ctx)
        self.pr = pr
        self.all = sb("distance_raw", [P, 4, KD, D], F32)
        self.raw = {n: self.all[:, i] for i, n in enumerate("voqk")}
        self.scratch = self.all[:, 0:2].rearrange("p n k d -> p n (k d)")
        self.bo_row = pr.bvo[0:1, :]
        self.bias_rows = sb("bias_rows", [3 * KD, P], F32)

    def load(self, sp):
        pr = self.pr
        for n, w in (("v", pr.Wv), ("o", pr.Wo), ("q", pr.Wq), ("k", pr.Wk)):
            sp.dma_start(self.raw[n], w.rearrange("(k p) n -> p k n", p=P)).then_inc(pr.s_dw, 16)
        for i, v in enumerate((pr.bq, pr.bk, pr.bv)):
            sp.dma_start(self.bias_rows[KD * i:KD * i + KD, :], v.rearrange("(k p) -> k p", p=P)).then_inc(pr.s_db, 16)
        sp.dma_start(self.bo_row, pr.bo.rearrange("(o d) -> o d", o=1)).then_inc(pr.s_db, 16)


class Norm:

    CHAIN = 11

    def __init__(self, pr, st, b):
        self.pr, self.b, self.parts = pr, b, 0
        self.s_stats, self.s_aggr, self.s_chain = pr.sems(st, f"stats{b}", f"aggr{b}", f"newton{b}")

    def stats(self, dve, t):
        dve.bn_stats(self.pr.stats[:, t, :], self.pr.x[:, self.b * TILES + t, :]).then_inc(self.s_stats, 1)

    def guess(self, dve, first=0, end=TILES):
        pr, b, self.cut = self.pr, self.b, slice(first, end)
        for t in range(first, end):
            dve.wait_ge(self.s_stats, t + 1)
            dve.bn_aggr(pr.mv[:, b, t, :], pr.stats[:, t, :]).then_inc(self.s_aggr, 1)
        dve.wait_ge(self.s_aggr, end)
        self.done = self.CHAIN * self.parts
        self.parts += 1
        v, y = pr.vare[:, self.cut], pr.rstd[:, b, self.cut]
        dve.tensor_scalar(v, pr.mv[:, b, self.cut, 1], EPS, None, ALU.add).then_inc(self.s_chain, 1)
        dve.wait_ge(self.s_chain, self.done + 1)
        dve.tensor_scalar(y.bitcast(I32), v.bitcast(I32), -0.5, float(0x5F3759DF), ALU.mult, ALU.add)\
           .then_inc(self.s_chain, 1)

    def newton(self, dve, i):
        pr, done = self.pr, self.done + 3 * i
        v, y, a, c = pr.vare[:, self.cut], pr.rstd[:, self.b, self.cut], pr.newton[:, 0, self.cut], pr.newton[:, 1, self.cut]
        dve.wait_ge(self.s_chain, done + 2)
        dve.scalar_tensor_tensor(out=a, in0=v, scalar=-0.5, in1=y, op0=ALU.mult, op1=ALU.mult).then_inc(self.s_chain, 1)
        dve.wait_ge(self.s_chain, done + 3)
        dve.tensor_tensor(c, a, y, ALU.mult).then_inc(self.s_chain, 1)
        dve.wait_ge(self.s_chain, done + 4)
        dve.scalar_tensor_tensor(out=y, in0=c, scalar=1.5, in1=y, op0=ALU.add, op1=ALU.mult).then_inc(self.s_chain, 1)
        if i == 2:
            dve.wait_ge(self.s_chain, self.CHAIN * self.parts)

    def rest(self, dve, first=0, end=TILES):
        self.guess(dve, first, end)
        for i in range(3):
            self.newton(dve, i)

    def whole(self, dve):
        for t in range(TILES):
            self.stats(dve, t)
        self.rest(dve)


class Routing:

    def __init__(self, pr, st, b, bank):
        self.pr, self.b, self.bank = pr, b, bank
        (self.s_shift, self.s_shifts, self.s_gathered, self.s_sum, self.s_pooled, self.s_logit, self.s_logits, self.s_best,
         self.s_chosen) = pr.sems(st, f"shift{b}", f"shifts{b}", f"gathered{b}", f"sum{b}", f"pooled{b}", f"logit{b}",
                                  f"logits{b}", f"best{b}", f"chosen{b}")

    def shift(self, dve):
        pr, b = self.pr, self.b
        dve.scalar_tensor_tensor(out=pr.shift[:], in0=pr.mv[:, b, :, 0], scalar=-1.0, in1=pr.rstd[:, b, :],
                                 op0=ALU.mult, op1=ALU.mult).then_inc(self.s_shift, 1)
        dve.wait_ge(self.s_shift, 1)
        dve.tensor_reduce(out=pr.shift_sum[:], in_=pr.shift[:], axis=AX.X, op=ALU.add).then_inc(self.s_shifts, 1)

    def gather(self, dve, t):
        pr, b = self.pr, self.b
        xt, rstd = pr.x[:, b * TILES + t, :], pr.rstd[:, b, t:t + 1]
        if t == 0:
            dve.wait_ge(self.s_shifts, 1)
            dve.tensor_scalar(pr.gathered[:], xt, rstd, pr.shift_sum[:], ALU.mult, ALU.add).then_inc(self.s_gathered, 1)
        else:
            dve.wait_ge(self.s_gathered, t)
            dve.scalar_tensor_tensor(out=pr.gathered[:], in0=xt, scalar=rstd, in1=pr.gathered[:], op0=ALU.mult, op1=ALU.add)\
               .then_inc(self.s_gathered, 1)

    def sums(self, pe):
        pe.wait_ge(self.s_gathered, TILES)
        for k in range(KD):
            mm = pe.matmul(self.bank[:, k:k + 1], self.pr.gathered[:, k * P:(k + 1) * P], self.pr.ones[:, 0:1], start=True, stop=True)
        mm.then_inc(self.s_sum, 1)

    def mean(self, dve):
        dve.wait_ge(self.s_sum, 1)
        dve.tensor_scalar(self.pr.pooled[:], self.bank[:, 0:KD], 1.0 / S, None, ALU.mult).then_inc(self.s_pooled, 1)

    def products(self, pe):
        pe.wait_ge(self.s_pooled, 1)
        pe.wait_ge(self.pr.s_wr, 16)
        for k in range(KD):
            mm = pe.matmul(self.bank[0:1, 0:E], self.pr.pooled[:, k:k + 1], self.pr.wr[:, k, :], start=(k == 0), stop=(k == KD - 1))
        mm.then_inc(self.s_logit, 1)

    def choose(self, dve):
        pr, b = self.pr, self.b
        dve.wait_ge(self.s_logit, 1)
        dve.tensor_copy(pr.logits[:], self.bank[0:1, 0:E]).then_inc(self.s_logits, 1)
        dve.wait_ge(self.s_logits, 1)
        dve.max(pr.best[:], pr.logits[:]).then_inc(self.s_best, 1)
        dve.wait_ge(self.s_best, 1)
        dve.max_index(pr.best_i[:, b, :], pr.best[:], pr.logits[:]).then_inc(self.s_chosen, 1)
        dve.tensor_tensor(pr.lead[0:1, b:b + 1], pr.best[0:1, 0:1], pr.best[0:1, 1:2], ALU.subtract).then_inc(self.s_chosen, 1)


def load_batch(pr, sp, b):
    for c in range(CHUNKS):
        sp.dma_start(pr.x[:, b * TILES + c * TPC:b * TILES + (c + 1) * TPC, :],
                     pr.x_d[b, c * CHUNK:(c + 1) * CHUNK, :].rearrange("(t p) d -> p t d", p=P)).then_inc(pr.s_x[b][c], 16)


def setup(pr):
    nc = pr.nc
    s_zero, s_made = pr.sems("setup", "zero", "made")
    with ExitStack() as ctx:
        block = ctx.enter_context(nc.Block())

        @block.sync
        def _(sp):
            load_batch(pr, sp, 0)

        @block.gpsimd
        def _(pool):
            pool.memset(pr.ident[:], 0.0).then_inc(s_zero, 1)
            pool.memset(pr.ident16[:], 0.0).then_inc(s_zero, 1)
            pool.memset(pr.ones[:], 1.0).then_inc(s_made, 1)
            pool.wait_ge(s_zero, 2)
            for m in (pr.ident, pr.ident16):
                pool.affine_select(out=m[:], in_=m[:], compare_op=ALU.not_equal, fill=1.0, base=0,
                                   pattern=[[-1, P]], channel_multiplier=1).then_inc(s_made, 1)


def head_attention(pr, distance_inputs):
    nc, x = pr.nc, pr.x
    GH = 4
    GD = GH * HD
    NG = NB * GROUPS
    with ExitStack() as ctx:
        sb, ps = pr.sb(ctx), pr.ps(ctx)
        values = sb("a_values", [P, 2, TILES, GH, 32], F32)
        moving = sb("a_moving", [P, 2, GH // 2, S], F16)
        fixed = sb("a_fixed", [P, 2, GH, S], F16)
        split_m = sb("a_split_m", [P, 2, TPC, GH, 2, 2, HD], F16)
        split_f = sb("a_split_f", [P, 2, TPC, GH, 2, 2, HD], F16)
        UR, SR = 8, 3
        probs = sb("a_probs", [P, UR, 2, CHUNK], F32)
        osb = sb("a_osb", [P, 2, CHUNK], F32)
        rden = sb("a_rden", [P, TPC, GH], F32)
        onorm = sb("a_onorm", [P, TPC, GH, HD], F32)
        scores = ps("a_scores", [P, 2 * SR, CHUNK], F32)
        spare = ps("a_out", [P, 2, CHUNK], F32)

        first_norm = Norm(pr, "a", 0)
        second_norm = Norm(pr, "a2", 1)
        next_norm = Norm(pr, "a3", 0)
        routing = Routing(pr, "a", 0, spare[:, 1, :])
        (s_zero, s_ones, s_xn, s_hi, s_lo_m, s_lo_f, s_tmov, s_tfix, s_emov, s_efix, s_scores, s_exp, s_mask, s_pv, s_ocopy,
         s_oturn, s_rden, s_onorm, s_added) = pr.sems(
            "a", "zero", "ones", "xn", "hi", "lo_m", "lo_f", "tmov", "tfix", "emov", "efix", "scores", "exp", "mask", "pv",
            "ocopy", "oturn", "rden", "onorm", "added")

        steps = [(G, c, kt) for G in range(NG) for c in range(CHUNKS) for kt in range(TPC * (c + 1))]
        outputs = [(G, c) for G in range(NG) for c in range(CHUNKS)]
        output_end, end = [], 0
        for G, c in outputs:
            end += TPC * (c + 1)
            output_end.append(end)
        GS = len(steps) // NG
        masked = [u for n, (G, c, kt) in enumerate(steps) if kt >= TPC * c for u in (2 * n, 2 * n + 1)]
        masks_by = [sum(1 for u in masked if u <= 2 * n + 1) for n in range(len(steps))]
        done = CHUNKS * GROUPS
        STATS_AT = {done + 1: range(TILES // 2), done + 3: range(TILES // 2, TILES)}
        NORM_AT = done + 5
        GATHER_AT = {done + 7: range(TILES // 2), done + 9: range(TILES // 2, TILES)}
        MEAN_AT, CHOOSE_AT = done + 9, done + 11

        def turned(job):
            G, cc = divmod(job, CHUNKS)
            return spare[:, 0 if cc >= 2 else 1, :].bitcast(F16)

        TURN_AT = {17: (0, 0), 19: (0, 1), 21: (1, 0), 23: (1, 1), 29: (2, 0), 31: (2, 1), 33: (3, 0), 35: (3, 1)}
        FIRST_TURN_AT = {8: (2, 0), 9: (2, 1), 10: (3, 0), 11: (3, 1)}

        def span(c, kt):
            skip = max(0, kt - TPC * c) * P
            return skip, CHUNK - skip

        with nc.Block() as block:
            @block.sync
            def _(sp):
                load_batch(pr, sp, 1)
                sp.dma_start(pr.wr[:], pr.Wr.rearrange("(k p) e -> p k e", p=P)).then_inc(pr.s_wr, 16)
                distance_inputs.load(sp)

            @block.vector
            def _(dve):
                def statistics(first, end):
                    for c in range(first, end):
                        dve.wait_ge(pr.s_x[0][c], 16)
                        for t in range(TPC * c, TPC * (c + 1)):
                            first_norm.stats(dve, t)
                    first_norm.rest(dve, TPC * first, TPC * end)

                def split(job):
                    G, cc = divmod(job, CHUNKS)
                    b, g = divmod(G, GROUPS)
                    if cc == 0 and G >= 2:
                        dve.wait_ge(s_pv, output_end[CHUNKS * (G - 1) - 1])
                    for t in range(TPC * cc, TPC * (cc + 1)):
                        dve.tensor_scalar(values[:, G % 2, t, :, 0:HD],
                                          x[:, b * TILES + t, GD * g:GD * (g + 1)].rearrange("p (h e) -> p h e", h=GH),
                                          pr.mv[:, b, t, 0:1], pr.rstd[:, b, t:t + 1], ALU.subtract, ALU.mult).then_inc(s_xn, 1)
                    if job >= 2:
                        dve.wait_ge(s_tmov, job - 1)
                        dve.wait_ge(s_tfix, job - 1)
                    dve.wait_ge(s_xn, TPC * (job + 1))
                    v = values[:, G % 2, TPC * cc:TPC * (cc + 1), :, 0:HD].rearrange("p t h e -> p (t h) e")
                    twice = v.unsqueeze(2).to_broadcast([P, TPC * GH, 2, HD])
                    m = split_m[:, job % 2].rearrange("p t h i j e -> p (t h) i j e")
                    f = split_f[:, job % 2].rearrange("p t h i j e -> p (t h) i j e")
                    dve.tensor_copy(f[:, :, 0, :, :], twice).then_inc(s_hi, 1)
                    dve.tensor_copy(m[:, :, :, 0, :], twice).then_inc(s_hi, 1)
                    dve.wait_ge(s_hi, 2 * job + 2)
                    dve.tensor_tensor(m[:, :, :, 1, :], twice, m[:, :, :, 0, :], ALU.subtract).then_inc(s_lo_m, 1)

                def place(job):
                    G, cc = divmod(job, CHUNKS)
                    cut = slice(cc * CHUNK, (cc + 1) * CHUNK)
                    dve.wait_ge(s_tmov, job + 1)
                    dve.tensor_copy(moving[:, G % 2, :, cut], turned(job).rearrange("p (r n) -> p r n", r=GH // 2)).then_inc(s_emov, 1)
                    dve.wait_ge(s_tfix, job + 1)
                    if job % CHUNKS == 0 and G < 2:
                        dve.wait_ge(s_zero, G + 1)
                    view = fixed[:, G % 2, :, cut].rearrange("p (r a) n -> p r a n", a=2)
                    src = turned(job).rearrange("p (r n) -> p r n", r=GH // 2)
                    dve.tensor_copy(view[0:64, :, 0, :], src[0:64]).then_inc(s_efix, 1)
                    dve.tensor_copy(view[64:128, :, 1, :], src[64:128]).then_inc(s_efix, 1)

                statistics(0, 1)
                split(0)
                statistics(1, 2)
                place(0)
                split(1)
                place(1)
                statistics(2, CHUNKS)
                split(2)
                split(3)
                for i, (G, c) in enumerate(outputs):
                    b, g = divmod(G, GROUPS)
                    if G + 1 < NG and c >= 2:
                        jobs = [CHUNKS * (G + 1) + 2 * (c - 2) + i for i in range(2)]
                        for job in jobs:
                            split(job)
                        for job in jobs:
                            place(job)
                    if i == 1:
                        place(2)
                        place(3)
                    if i == CHUNKS + 1:
                        for s_chunk in pr.s_x[1]:
                            dve.wait_ge(s_chunk, 16)
                        second_norm.whole(dve)
                    if i in STATS_AT:
                        dve.wait_ge(s_added, CHUNKS * GROUPS)
                        for t in STATS_AT[i]:
                            next_norm.stats(dve, t)
                    if i == NORM_AT:
                        next_norm.rest(dve)
                        routing.shift(dve)
                    for t in GATHER_AT.get(i, ()):
                        routing.gather(dve, t)
                    dve.wait_ge(s_pv, output_end[i])
                    dve.tensor_copy(osb[:, i % 2, :], spare[:, i % 2, :]).then_inc(s_ocopy, 1)
                    dve.wait_ge(s_oturn, i + 1)
                    o = spare[:, i % 2, :].rearrange("p (t j e) -> p t j e", t=TPC, j=GH)
                    dve.reciprocal(rden[:], o[:, :, :, HD]).then_inc(s_rden, 1)
                    dve.wait_ge(s_rden, i + 1)
                    dve.tensor_tensor(onorm[:], o[:, :, :, 0:HD], rden[:].unsqueeze(3).to_broadcast([P, TPC, GH, HD]),
                                      ALU.mult).then_inc(s_onorm, 1)
                    dve.wait_ge(s_onorm, i + 1)
                    xv = x[:, b * TILES + c * TPC:b * TILES + (c + 1) * TPC, GD * g:GD * (g + 1)]\
                        .rearrange("p t (j e) -> p t j e", j=GH)
                    dve.tensor_tensor(xv, xv, onorm[:], ALU.add).then_inc(s_added, 1)
                    if i == MEAN_AT:
                        routing.mean(dve)
                    if i == CHOOSE_AT:
                        routing.choose(dve)

            @block.scalar
            def _(act):
                for n, (G, c, kt) in enumerate(steps):
                    skip, w = span(c, kt)
                    for a in range(2):
                        u = 2 * n + a
                        act.wait_ge(s_scores, u + 1)
                        if u >= UR:
                            act.wait_ge(s_pv, (u - UR) // 2 + 1)
                        act.activation(probs[:, u % UR, :, 0:w], scores[:, 2 * (u % SR):2 * (u % SR) + 2, 0:w], ACT.Exp,
                                       scale=HD ** -0.5).then_inc(s_exp, 1)

            @block.gpsimd
            def _(pool):
                pool.memset(fixed[:, 0].bitcast(F32), 0.0).then_inc(s_zero, 1)

                def split_low(job):
                    G, cc = divmod(job, CHUNKS)
                    pool.wait_ge(s_hi, 2 * job + 2)
                    v = values[:, G % 2, TPC * cc:TPC * (cc + 1), :, 0:HD].rearrange("p t h e -> p (t h) e")
                    f = split_f[:, job % 2].rearrange("p t h i j e -> p (t h) i j e")
                    pool.tensor_tensor(f[:, :, 1, :, :], v.unsqueeze(2).to_broadcast([P, TPC * GH, 2, HD]), f[:, :, 0, :, :],
                                       ALU.subtract).then_inc(s_lo_f, 1)

                split_low(0)
                pool.memset(values[:, :, :, :, HD:32].rearrange("p s t h e -> p (s t h) e"), 1.0).then_inc(s_ones, 1)
                split_low(1)
                for n, (G, c, kt) in enumerate(steps):
                    if n in (TPC, TPC + 2):
                        split_low(2 + (n - TPC) // 2)
                    if n == 3 * TPC:
                        pool.memset(fixed[:, 1].bitcast(F32), 0.0).then_inc(s_zero, 1)
                    if kt >= TPC * c:
                        for u in (2 * n, 2 * n + 1):
                            pool.wait_ge(s_exp, u + 1)
                            tri = probs[:, u % UR, :, 0:P]
                            pool.affine_select(out=tri, in_=tri, compare_op=ALU.is_ge, fill=0.0, base=0,
                                               pattern=[[0, 2], [1, P]], channel_multiplier=-1).then_inc(s_mask, 1)
                    if n % GS + 1 in TURN_AT and TURN_AT[n % GS + 1][1] == 0 and G + 1 < NG:
                        split_low(CHUNKS * (G + 1) + TURN_AT[n % GS + 1][0])

            @block.tensor
            def _(pe):
                turns = [0, 0]
                routed = []

                def spare_free():
                    sides, outs = turns
                    if sides:
                        pe.wait_ge(s_emov, (sides + 1) // 2)
                        pe.wait_ge(s_efix, 2 * (sides // 2))
                    if outs:
                        pe.wait_ge(s_added, outs)
                    for s_read in routed:
                        pe.wait_ge(s_read, 1)
                    routed.clear()

                def turn(job, side):
                    spare_free()
                    if side == 0:
                        pe.wait_ge(s_lo_m, job + 1)
                    else:
                        pe.wait_ge(s_lo_f, job + 1)
                    split, turned_job = ((split_m, s_tmov), (split_f, s_tfix))[side]
                    for t in range(TPC):
                        for r in range(GH // 2):
                            mm = pe.transpose(turned(job)[:, (r * TPC + t) * P:(r * TPC + t + 1) * P],
                                              split[:, job % 2, t, 2 * r:2 * r + 2].rearrange("p a i j e -> p (a i j e)"),
                                              pr.ident16[:])
                    mm.then_inc(turned_job, 1)
                    turns[0] += 1

                def turn_out(i):
                    spare_free()
                    pe.wait_ge(s_ocopy, i + 1)
                    for t in range(TPC):
                        mm = pe.transpose(spare[:, i % 2, t * P:(t + 1) * P], osb[:, i % 2, t * P:(t + 1) * P], pr.ident[:])
                    mm.then_inc(s_oturn, 1)
                    turns[1] += 1

                def products(n):
                    G, c, kt = steps[n]
                    i = CHUNKS * G + c
                    skip, w = span(c, kt)
                    if kt == 0:
                        spare_free()
                    pe.wait_ge(s_exp, 2 * n + 2)
                    pe.wait_ge(s_mask, masks_by[n])
                    for j in range(GH):
                        mm = pe.matmul(spare[32 * j:32 * j + 32, i % 2, skip:CHUNK], values[:, G % 2, kt, j, :],
                                       probs[:, (2 * n + j // 2) % UR, j % 2, 0:w], start=(kt == 0),
                                       stop=(kt == TPC * (c + 1) - 1), skip_group_check=True)
                    mm.then_inc(s_pv, 1)

                for job in range(2):
                    for side in range(2):
                        turn(job, side)
                pe.wait_ge(s_ones, 1)
                turned_outputs = 0
                LAG = 2
                for n, (G, c, kt) in enumerate(steps):
                    skip, w = span(c, kt)
                    q0 = c * CHUNK + skip
                    if kt == 0:
                        pe.wait_ge(s_emov, CHUNKS * G + c + 1)
                        pe.wait_ge(s_efix, 2 * (CHUNKS * G + c + 1))
                    for a in range(2):
                        u = 2 * n + a
                        if u >= SR:
                            pe.wait_ge(s_exp, u - SR + 1)
                        for h in range(2):
                            mm = pe.matmul(scores[:, 2 * (u % SR) + h, 0:w], fixed[:, G % 2, 2 * a + h, kt * P:(kt + 1) * P],
                                           moving[:, G % 2, a, q0:q0 + w], start=True, stop=True)
                        mm.then_inc(s_scores, 1)
                    if n >= LAG:
                        products(n - LAG)
                    if turned_outputs < len(outputs) and n == output_end[turned_outputs] + LAG + 1:
                        turn_out(turned_outputs)
                        turned_outputs += 1
                    if turned_outputs and n == output_end[turned_outputs - 1] + LAG + 2:
                        if turned_outputs - 1 == MEAN_AT:
                            spare_free()
                            routing.sums(pe)
                            routed.append(routing.s_pooled)
                        if turned_outputs - 1 == CHOOSE_AT:
                            spare_free()
                            routing.products(pe)
                            routed.append(routing.s_logits)
                    if G == 0 and n in FIRST_TURN_AT:
                        turn(*FIRST_TURN_AT[n])
                    if n % GS in TURN_AT and G + 1 < NG:
                        job, side = TURN_AT[n % GS]
                        turn(CHUNKS * (G + 1) + job, side)
                for n in range(len(steps) - LAG, len(steps)):
                    products(n)
                for i in range(turned_outputs, len(outputs)):
                    turn_out(i)


class NormedColumns:

    RING = 4

    def __init__(self, pr, st, sb, banks, second=None):
        self.pr, self.banks, self.second = pr, banks, second
        self.xn = sb(f"{st}_xn", [P, self.RING, D], F32)
        self.hi = sb(f"{st}_xhi", [P, KD, S], F32R)
        self.lo = sb(f"{st}_xlo", [P, KD, S], F32R)
        self.s_xn, self.s_turn, self.s_hi, self.s_lo = pr.sems(st, "xn", "turn", "xhi", "xlo")

    def bank(self, use):
        bank = self.second if self.second is not None and use == 1 else self.banks[use % len(self.banks)]
        return bank.rearrange("p (k n) -> p k n", k=KD)

    def norm(self, dve, use, b, pair):
        if use >= self.RING // 2:
            dve.wait_ge(self.s_turn, use - self.RING // 2 + 1)
        for i in range(2):
            t = 2 * pair + i
            dve.tensor_scalar(self.xn[:, (2 * use + i) % self.RING, :], self.pr.x[:, b * TILES + t, :],
                              self.pr.mv[:, b, t, 0:1], self.pr.rstd[:, b, t:t + 1], ALU.subtract, ALU.mult)\
               .then_inc(self.s_xn, 1)

    def turn(self, pe, use):
        n = len(self.banks)
        if use >= n and not (use == 1 and self.second is not None):
            pe.wait_ge(self.s_lo, use - n + 1)
        pe.wait_ge(self.s_xn, 2 * use + 2)
        for i in range(2):
            for k in range(KD):
                mm = pe.transpose(self.bank(use)[:, k, i * P:(i + 1) * P],
                                  self.xn[:, (2 * use + i) % self.RING, k * P:(k + 1) * P], self.pr.ident[:])
        mm.then_inc(self.s_turn, 1)

    def high(self, act, use, pair):
        act.wait_ge(self.s_turn, use + 1)
        act.activation(self.hi[:, :, 2 * P * pair:2 * P * (pair + 1)], self.bank(use), ACT.Copy).then_inc(self.s_hi, 1)

    def low(self, dve, use, pair):
        dve.wait_ge(self.s_hi, use + 1)
        cols = slice(2 * P * pair, 2 * P * (pair + 1))
        dve.tensor_tensor(self.lo[:, :, cols], self.bank(use), self.hi[:, :, cols].bitcast(F32), ALU.subtract)\
           .then_inc(self.s_lo, 1)


def split_product(pe, out, fixed_hi, fixed_lo, moving_hi, moving_lo, first, last):
    pe.matmul(out, fixed_hi, moving_hi, start=first, stop=False)
    pe.matmul(out, fixed_hi, moving_lo, start=False, stop=False)
    return pe.matmul(out, fixed_lo, moving_hi, start=False, stop=last)


def add_columns(pr, st, turn_bank, b=0, scale=None):
    s_turned, s_added = pr.sems(st, "result_turned", "result_added")

    def tensor(pe, c, half, result, s_result):
        n = c * (TPC // 2) + half
        pe.wait_ge(s_result, KD * (c + 1))
        if n >= 1:
            pe.wait_ge(s_added, n)
        for t in range(2):
            for k in range(KD):
                q = (2 * half + t) * P
                mm = pe.transpose(turn_bank[:, (t * KD + k) * P:(t * KD + k + 1) * P], result[:, k, q:q + P], pr.ident[:])
        mm.then_inc(s_turned, 1)

    def vector(dve, c, half):
        n = c * (TPC // 2) + half
        dve.wait_ge(s_turned, n + 1)
        xv = pr.x[:, b * TILES + c * TPC + 2 * half:b * TILES + c * TPC + 2 * half + 2, :]
        turned = turn_bank[:].rearrange("p (t d) -> p t d", t=2)
        if scale is None:
            dve.tensor_tensor(xv, xv, turned, ALU.add).then_inc(s_added, 1)
        else:
            for t in range(2):
                add = dve.scalar_tensor_tensor(out=xv[:, t], in0=turned[:, t], scalar=scale[:, c % 2, 2 * half + t:2 * half + t + 1],
                                               in1=xv[:, t], op0=ALU.mult, op1=ALU.add)
            add.then_inc(s_added, 1)

    return tensor, vector, s_turned, s_added


def mixture(pr, layer, last_layer):
    nc = pr.nc
    st = f"f{layer}"
    with ExitStack() as ctx:
        sb, ps = pr.sb(ctx), pr.ps(ctx)
        raw1 = sb(f"{st}_raw1", [P, TOPK, KD, F], F32)
        raw2 = sb(f"{st}_raw2", [P, TOPK, FT, D], F32)
        w1h = sb(f"{st}_w1h", [P, TOPK, KD, F], F32R)
        w1l = sb(f"{st}_w1l", [P, TOPK, KD, F], F32R)
        w2h = sb(f"{st}_w2h", [P, TOPK, FT, D], F32R)
        w2l = sb(f"{st}_w2l", [P, TOPK, FT, D], F32R)
        HR, LAG = 4, 3
        gel = sb(f"{st}_gelu", [P, HR, CHUNK], F32)
        hh = sb(f"{st}_hh", [P, HR, CHUNK], F32R)
        hl = sb(f"{st}_hl", [P, HR, CHUNK], F32R)
        ysb = sb(f"{st}_y", [P, KD, CHUNK], F32)
        BR = TOPK * (FT + KD)
        brow = sb(f"{st}_brow", [BR, P], F32)
        bcol = sb(f"{st}_bcol", [P, NB, BR], F32)
        b2w = sb(f"{st}_b2w", [P, NB, 2, KD], F32)
        gate = sb(f"{st}_gate", [1, 8], F32)
        gates = sb(f"{st}_gates", [P, NB, TOPK], F32)
        hps = ps(f"{st}_h", [P, 2, CHUNK], F32)
        yps = ps(f"{st}_ypsum", [P, 2 * KD, CHUNK], F32)
        misc = ps(f"{st}_misc", [P, CHUNK], F32)
        side = ps(f"{st}_side", [P, CHUNK], F32)
        cols = NormedColumns(pr, st, sb, [side[:]], second=misc[:])
        norms = {b: Norm(pr, st, b) for b in range(NB)}
        routing = Routing(pr, st, 1, side)

        s_tanh, s_gate, s_spread, s_gates, s_b2w, s_bturn, s_bcol = pr.sems(
            st, "tanh", "gate", "spread", "gates", "b2w", "bturn", "bcol")
        s_braw, s_wh, s_wl, s_h, s_gelu, s_hh, s_hl, s_used, s_y = pr.sems(
            st, "braw", "wh", "wl", "h", "gelu", "hh", "hl", "used", "y")
        s_raw = pr.sems(st, *[f"raw{w}_{e}_{half}" for e in range(TOPK) for half in range(2) for w in (1, 2)])
        add_tensor, add_vector, s_rturned, s_added = add_columns(pr, st, misc)

        CS = TOPK * FT
        BS = CHUNKS * CS
        steps = [(q, c, e, j) for q in range(NB) for c in range(CHUNKS) for e in range(TOPK) for j in range(FT)]
        WP = 16

        def part(i):
            e, k, w = i // 8, i % 8 // 2, i % 2
            if w == 0:
                views = [m[:, e, :, 256 * k:256 * k + 256] for m in (raw1, w1h, w1l)]
            else:
                views = [m[:, e, 2 * k:2 * k + 2, :] for m in (raw2, w2h, w2l)]
            return s_raw[4 * e + 2 * (k // 2) + w], views

        def beside(n):
            q, at = divmod(n, BS)
            work = []
            c, a = divmod(at, CS)
            last_batch = q == NB - 1
            if not (last_batch and c == CHUNKS - 1):
                first = {7: 0, 10: 1}
                pair = lambda i: (q, 2 * (c + 1) + i) if c < CHUNKS - 1 else (q + 1, i)
                for f, i in first.items():
                    if f <= a <= f + 2:
                        work.append((("norm", "turn", "low")[a - f], pair(i)))
            if not last_batch:
                if at < 16:
                    work.append(("stats", (1, at)))
                if at == 16:
                    work.append(("norms", 1))
                if 17 <= at < 17 + TILES:
                    work.append(("gather", at - 17))
                work += [(kind, q + 1) for kind, when in
                         (("sums", 34), ("mean", 35), ("logits", 36), ("choose", 37), ("tanh", 38), ("gate", 44), ("spread", 45), ("gates", 46),
                          ("turn_biases", 47), ("biases", 48)) if at == when]
                if 56 <= at:
                    work.append(("weights", (q + 1, at - 56)))
            else:
                if at < 16:
                    work.append(("stats", (0, at)))
                if at == 16:
                    work.append(("norms", 0))
            ahead = AHEAD if q == 0 else 8
            if at < WP - ahead:
                work.append(("weights", (q, ahead + at)))
            return work

        AHEAD = 2
        before = [("norm", (0, 0)), ("norm", (0, 1)), ("turn", (0, 0)), ("turn", (0, 1)), ("low", (0, 0)), ("low", (0, 1)),
                  ("tanh", 0), ("gate", 0), ("spread", 0), ("gates", 0), ("turn_biases", 0), ("biases", 0)]
        before += [("weights", (0, i)) for i in range(AHEAD)]

        with nc.Block() as block:
            @block.sync
            def _(sp):
                for q in range(NB):
                    if q == 1:
                        sp.wait_ge(routing.s_chosen, 2)
                    chosen = [sp.value_load(pr.best_i[0:1, q, e:e + 1], min_val=0, max_val=E - 1) for e in range(TOPK)]
                    if q >= 1:
                        sp.wait_ge(s_bturn, q)
                    for e, n in enumerate(chosen):
                        o = TOPK * FT + KD * e
                        sp.dma_start(brow[FT * e:FT * e + FT, :], pr.b1[bass.ds(n, 1)].rearrange("o (j p) -> (o j) p", p=P)).then_inc(s_braw, 16)
                        sp.dma_start(brow[o:o + KD, :], pr.b2[bass.ds(n, 1)].rearrange("o (k p) -> (o k) p", p=P)).then_inc(s_braw, 16)
                    for e, n in enumerate(chosen):
                        for half in range(2):
                            units = slice(half * F // 2, (half + 1) * F // 2)
                            if q >= 1:
                                sp.wait_ge(s_wl, WP * (q - 1) + 8 * e + 4 * half + 4)
                            sp.dma_start(raw1[:, e, :, units], pr.W1[bass.ds(n, 1), :, units].rearrange("o (k p) f -> p (o k) f", p=P))\
                              .then_inc(s_raw[4 * e + 2 * half], 16)
                            sp.dma_start(raw2[:, e, half * FT // 2:(half + 1) * FT // 2, :],
                                         pr.W2[bass.ds(n, 1), units, :].rearrange("o (j p) d -> p (o j) d", p=P))\
                              .then_inc(s_raw[4 * e + 2 * half + 1], 16)
                if last_layer:
                    for chunk in range(NB * CHUNKS):
                        b, c = divmod(chunk, CHUNKS)
                        sp.wait_ge(s_added, (TPC // 2) * (chunk + 1))
                        sp.dma_start(pr.out_d[b, c * CHUNK:(c + 1) * CHUNK, :].rearrange("(t p) d -> p t d", p=P),
                                     pr.x[:, chunk * TPC:(chunk + 1) * TPC, :]).then_inc(pr.s_out, 16)
                    sp.wait_ge(pr.s_out, 16 * NB * CHUNKS)

            @block.tensor
            def _(pe):
                use = [0]
                side_reads = []

                def side_free():
                    for s_read, count in side_reads:
                        pe.wait_ge(s_read, count)
                    side_reads.clear()

                def do(kind, what):
                    if kind == "turn":
                        side_free()
                        cols.turn(pe, use[0])
                        use[0] += 1
                        return
                    if kind == "sums":
                        pe.wait_ge(cols.s_lo, use[0])
                        side_free()
                        routing.sums(pe)
                    elif kind == "logits":
                        routing.products(pe)
                        side_reads.append((routing.s_logits, 1))
                    elif kind == "spread":
                        pe.wait_ge(s_gate, what + 1)
                        pe.wait_ge(cols.s_lo, use[0])
                        side_free()
                        pe.matmul(side[:, 0:TOPK], pr.ones[0:1, :], gate[0:1, 4:4 + TOPK], start=True, stop=True).then_inc(s_spread, 1)
                        side_reads.append((s_gates, what + 1))
                    elif kind == "turn_biases":
                        pe.wait_ge(s_braw, 4 * 16 * (what + 1))
                        pe.wait_ge(cols.s_lo, use[0])
                        side_free()
                        pe.transpose(side[:, 0:BR], brow[:], pr.ident[0:BR, 0:BR]).then_inc(s_bturn, 1)
                        side_reads.append((s_bcol, what + 1))

                def up(n):
                    q, c, e, j = steps[n]
                    if c == 0:
                        pe.wait_ge(s_wl, WP * q + 8 * e + 2 * (j // 2) + 1)
                    if e == 0 and j == 0:
                        pe.wait_ge(cols.s_lo, (TILES // 2) * q + 2 * (c + 1))
                    if n >= 2:
                        pe.wait_ge(s_gelu, n - 1)
                    for k in range(KD):
                        mm = split_product(pe, hps[:, n % 2, :], w1h[:, e, k, j * P:(j + 1) * P], w1l[:, e, k, j * P:(j + 1) * P],
                                           cols.hi[:, k, c * CHUNK:(c + 1) * CHUNK], cols.lo[:, k, c * CHUNK:(c + 1) * CHUNK],
                                           k == 0, k == KD - 1)
                    mm.then_inc(s_h, 1)

                def down(n):
                    q, c, e, j = steps[n]
                    chunk = CHUNKS * q + c
                    if c == 0:
                        pe.wait_ge(s_wl, WP * q + 8 * e + 2 * (j // 2) + 2)
                    if e == 0 and j == 0 and chunk >= 2:
                        pe.wait_ge(s_y, KD * (chunk - 1))
                    pe.wait_ge(s_hl, n + 1)
                    for k in range(KD):
                        mm = split_product(pe, yps[:, KD * (chunk % 2) + k, :], w2h[:, e, j, k * P:(k + 1) * P],
                                           w2l[:, e, j, k * P:(k + 1) * P], hh[:, n % HR, :], hl[:, n % HR, :],
                                           e == 0 and j == 0, e == TOPK - 1 and j == FT - 1)
                    mm.then_inc(s_used, 1)

                for work in before:
                    do(*work)
                for n in range(len(steps) + LAG):
                    if n < len(steps):
                        up(n)
                    if n >= LAG:
                        down(n - LAG)
                    chunk, at = divmod(n, CS)
                    if 1 <= chunk < NB * CHUNKS and at in (4, 6):
                        add_tensor(pe, chunk - 1, (at - 4) // 2, ysb, s_y)
                    if n < len(steps):
                        for work in beside(n):
                            do(*work)
                for half in range(2):
                    add_tensor(pe, NB * CHUNKS - 1, half, ysb, s_y)

            @block.scalar
            def _(act):
                use = [0]

                def do(kind, what):
                    if kind == "turn":
                        cols.high(act, use[0], what[1])
                        use[0] += 1
                    elif kind == "tanh":
                        if what == 1:
                            act.wait_ge(routing.s_chosen, 2)
                            act.wait_ge(s_gate, 1)
                        lead = pr.lead[0:1, what:what + 1]
                        act.activation(gate[0:1, 2:3], lead, ACT.Tanh, scale=0.5).then_inc(s_tanh, 1)
                        act.activation(gate[0:1, 3:4], lead, ACT.Tanh, scale=-0.5).then_inc(s_tanh, 1)
                    elif kind == "weights":
                        q, i = what
                        arrived, (raw, hi, lo) = part(i)
                        act.wait_ge(arrived, 16 * (q + 1))
                        if q >= 1:
                            last = (q - 1) * BS + (CHUNKS - 1) * CS + FT * (i // 8) + 2 * (i % 8 // 2) + 2
                            act.wait_ge((s_h, s_used)[i % 2], last)
                        act.activation(hi, raw, ACT.Copy).then_inc(s_wh, 1)

                for work in before:
                    do(*work)
                for n, (q, c, e, j) in enumerate(steps):
                    if c == 0 and e == 0 and j == 0:
                        act.wait_ge(s_bcol, q + 1)
                    act.wait_ge(s_h, n + 1)
                    if n >= HR:
                        act.wait_ge(s_hl, n - HR + 1)
                    act.activation(gel[:, n % HR, :], hps[:, n % 2, :], ACT.Gelu, bias=bcol[:, q, FT * e + j:FT * e + j + 1])\
                       .then_inc(s_gelu, 1)
                    for work in beside(n):
                        do(*work)

            @block.vector
            def _(dve):
                normed, lows = [0], [0]

                def do(kind, what):
                    if kind == "norm":
                        q, pair = what
                        cols.norm(dve, normed[0], q, pair)
                        normed[0] += 1
                    elif kind == "low":
                        q, pair = what
                        cols.low(dve, lows[0], pair)
                        lows[0] += 1
                    elif kind == "stats":
                        norms[what[0]].stats(dve, what[1])
                    elif kind == "norms":
                        norms[what].rest(dve)
                        if what == 1:
                            routing.shift(dve)
                    elif kind == "gather":
                        routing.gather(dve, what)
                    elif kind == "mean":
                        routing.mean(dve)
                    elif kind == "choose":
                        routing.choose(dve)
                    elif kind == "gate":
                        q = what
                        dve.wait_ge(s_tanh, 2 * (q + 1))
                        dve.tensor_scalar(gate[0:1, 4:6], gate[0:1, 2:4], 0.5, 0.5, ALU.mult, ALU.add).then_inc(s_gate, 1)
                    elif kind == "gates":
                        q = what
                        dve.wait_ge(s_spread, q + 1)
                        dve.tensor_copy(gates[:, q, :], side[:, 0:TOPK]).then_inc(s_gates, 1)
                    elif kind == "biases":
                        q = what
                        dve.wait_ge(s_bturn, q + 1)
                        dve.tensor_copy(bcol[:, q, :], side[:, 0:BR]).then_inc(s_bcol, 1)
                        dve.wait_ge(s_bcol, q + 1)
                        dve.wait_ge(s_gates, q + 1)
                        o = TOPK * FT
                        dve.tensor_scalar(b2w[:, q, 0, :], bcol[:, q, o:o + KD], gates[:, q, 0:1], None, ALU.mult).then_inc(s_b2w, 1)
                        dve.wait_ge(s_b2w, 2 * q + 1)
                        dve.scalar_tensor_tensor(out=b2w[:, q, 1, :], in0=bcol[:, q, o + KD:o + 2 * KD], scalar=gates[:, q, 1:2],
                                                 in1=b2w[:, q, 0, :], op0=ALU.mult, op1=ALU.add).then_inc(s_b2w, 1)
                    elif kind == "weights":
                        q, i = what
                        arrived, (raw, hi, lo) = part(i)
                        dve.wait_ge(s_wh, WP * q + i + 1)
                        dve.tensor_tensor(lo, raw, hi.bitcast(F32), ALU.subtract).then_inc(s_wl, 1)

                def result(chunk):
                    q = chunk // CHUNKS
                    dve.wait_ge(s_used, (chunk + 1) * CS)
                    dve.wait_ge(s_b2w, 2 * (q + 1))
                    if chunk >= 1:
                        dve.wait_ge(s_rturned, (TPC // 2) * chunk)
                    for k in range(KD):
                        dve.tensor_scalar(ysb[:, k, :], yps[:, KD * (chunk % 2) + k, :], b2w[:, q, 1, k:k + 1], None, ALU.add)\
                           .then_inc(s_y, 1)

                for work in before:
                    do(*work)
                for n, (q, c, e, j) in enumerate(steps):
                    dve.wait_ge(s_gelu, n + 1)
                    if n >= HR:
                        dve.wait_ge(s_used, n - HR + 1)
                    dve.tensor_scalar(hh[:, n % HR, :], gel[:, n % HR, :], gates[:, q, e:e + 1], None, ALU.mult).then_inc(s_hh, 1)
                    dve.wait_ge(s_hh, n + 1)
                    dve.scalar_tensor_tensor(out=hl[:, n % HR, :], in0=gel[:, n % HR, :], scalar=gates[:, q, e:e + 1],
                                             in1=hh[:, n % HR, :].bitcast(F32), op0=ALU.mult, op1=ALU.subtract).then_inc(s_hl, 1)
                    chunk, at = divmod(n, CS)
                    if chunk >= 1 and at == 3:
                        result(chunk - 1)
                    if chunk >= 1 and at in (5, 6):
                        add_vector(dve, chunk - 1, at - 5)
                    for work in beside(n):
                        do(*work)
                result(NB * CHUNKS - 1)
                for half in range(2):
                    add_vector(dve, NB * CHUNKS - 1, half)


class DistanceWeights:

    def __init__(self, pr, ctx, inputs):
        nc = pr.nc
        sb = pr.sb(ctx)
        self.hi, self.lo, self.scratch = {}, {}, inputs.scratch
        for name in ("q", "k", "vo"):
            self.hi[name] = sb(f"w{name}_hi", [P, KD, D], F32R)
            self.lo[name] = sb(f"w{name}_lo", [P, KD, D], F32R)
        s_vturn, s_vcol, s_vo, s_bvo, s_vo32, s_hi, s_lo, s_bias = pr.sems(
            "dw", "vturn", "vcol", "vo", "bvo", "vo32", "hi", "lo", "bias")
        (s_wide,) = pr.sems("dw", "wide")
        with ExitStack() as tmp:
            tsb, ps = pr.sb(tmp), pr.ps(tmp)
            raw = dict(inputs.raw, vo=tsb("wvo_raw", [P, KD, D], F32)[:])
            vcol = tsb("wv_turned", [P, KD, D], F32)
            turn = ps("dw_turn", [P, KD, D], F32)
            prod = ps("dw_prod", [P, KD, D], F32)
            bias = ps("dw_bias", [P, D], F32)
            bv_wide = tsb("bv_wide", [P, KD, P], F32)
            bias_cols = ps("dw_bias_cols", [P, 3 * KD], F32)
            s_cols, s_bias_b = pr.sems("dw", "cols", "bias_b")
            block = tmp.enter_context(nc.Block())

            @block.tensor
            def _(pe):
                pe.wait_ge(pr.s_db, 4 * 16)
                pe.wait_ge(pr.s_dw, 4 * 16)
                pe.transpose(bias_cols[:], inputs.bias_rows[:], pr.ident[0:3 * KD, 0:3 * KD]).then_inc(s_cols, 1)
                for r in range(KD):
                    for k in range(KD):
                        mm = pe.transpose(turn[:, k, r * P:(r + 1) * P], raw["v"][:, r, k * P:(k + 1) * P], pr.ident[:])
                mm.then_inc(s_vturn, 1)
                pe.wait_ge(s_vcol, 1)
                for r in range(KD):
                    for k in range(KD):
                        mm = pe.matmul(prod[:, r, :], vcol[:, k, r * P:(r + 1) * P], raw["o"][:, k, :],
                                       start=(k == 0), stop=(k == KD - 1))
                mm.then_inc(s_vo, 1)
                pe.wait_ge(s_wide, KD)
                for k in range(KD):
                    pe.matmul(bias[:], bv_wide[:, k, :], raw["o"][:, k, :], start=(k == 0), stop=False)
                pe.matmul(bias[:], pr.ones[0:1, :], inputs.bo_row, start=False, stop=True).then_inc(s_bvo, 1)

            @block.vector
            def _(dve):
                dve.wait_ge(s_cols, 1)
                dve.tensor_copy(pr.bias_b[:].rearrange("p i k -> p (i k)"), bias_cols[:]).then_inc(s_bias_b, 1)
                dve.wait_ge(s_bias_b, 1)
                for k in range(KD):
                    dve.tensor_scalar(bv_wide[:, k, :], pr.ones[:], pr.bias_b[:, 2, k:k + 1], None, ALU.mult).then_inc(s_wide, 1)
                dve.wait_ge(s_vturn, 1)
                dve.tensor_copy(vcol[:], turn[:]).then_inc(s_vcol, 1)
                dve.wait_ge(pr.s_dw, 4 * 16)
                for i, n in enumerate(("q", "k", "vo")):
                    if n == "vo":
                        dve.wait_ge(s_vo, 1)
                        dve.tensor_copy(raw["vo"], prod[:]).then_inc(s_vo32, 1)
                        dve.wait_ge(s_vo32, 1)
                    dve.tensor_copy(self.hi[n][:], raw[n]).then_inc(s_hi, 1)
                    dve.wait_ge(s_hi, i + 1)
                    dve.tensor_tensor(self.lo[n][:], raw[n], self.hi[n][:].bitcast(F32), ALU.subtract).then_inc(s_lo, 1)
                dve.wait_ge(s_bvo, 1)
                dve.tensor_copy(pr.bvo[:], bias[:]).then_inc(s_bias, 1)


def distance_attention(pr, b, w):
    nc = pr.nc
    st = f"b{b}"
    with ExitStack() as ctx:
        sb, ps = pr.sb(ctx), pr.ps(ctx)
        hi = {n: sb(f"{st}_{n}hi", [P, KD, S], F32R) for n in "qk"}
        lo = {n: sb(f"{st}_{n}lo", [P, KD, S], F32R) for n in "qk"}
        vhi = sb(f"{st}_vhi", [P, TILES, D], F32R)
        vlo = sb(f"{st}_vlo", [P, TILES, D], F32R)
        qsq = sb(f"{st}_qsq", [P, S], F32)
        nksq = sb(f"{st}_nksq", [P, TILES], F32)
        banks = ps(f"{st}_banks", [P, 3, CHUNK], F32)
        outs = ps(f"{st}_outs", [P, 2 * KD, CHUNK], F32)
        misc = ps(f"{st}_misc", [P, CHUNK], F32)

        with ExitStack() as part:
            psb = pr.sb(part)
            cols = NormedColumns(pr, st, psb, [banks[:, i, :] for i in range(2)])
            vbank = banks[:, 2, :]
            qk32 = psb(f"{st}_qk32", [P, 2, KD, CHUNK], F32)
            square = w.scratch
            s_v, s_vhi, s_vlo, s_p, s_p32, s_phi, s_plo, s_sq, s_len, s_lenc = pr.sems(
                st, "v", "vhi", "vlo", "p", "p32", "phi", "plo", "sq", "len", "lenc")
            s_xb, s_sqsum = pr.sems(st, "x_biased", "sqsum")
            tasks = [(n, c) for c in range(CHUNKS) for n in "kq"]
            with nc.Block() as block:
                @block.tensor
                def _(pe):
                    def values(u):
                        pe.wait_ge(cols.s_lo, u + 1)
                        if u >= 1:
                            pe.wait_ge(s_vlo, u)
                        for t in (2 * u, 2 * u + 1):
                            for k in range(KD):
                                tok = slice(t * P, (t + 1) * P)
                                mm = split_product(pe, vbank[:, (t % 2) * D:(t % 2 + 1) * D], cols.hi[:, k, tok], cols.lo[:, k, tok],
                                                   w.hi["vo"][:, k, :], w.lo["vo"][:, k, :], k == 0, k == KD - 1)
                        mm.then_inc(s_v, 1)

                    def project(i):
                        n, c = tasks[i]
                        pe.wait_ge(cols.s_lo, 2 * (c + 1))
                        for m in range(KD):
                            j = KD * i + m
                            if j >= 4:
                                pe.wait_ge(s_sq, j - 3)
                            for k in range(KD):
                                mm = split_product(pe, outs[:, j % 4, :], w.hi[n][:, k, m * P:(m + 1) * P],
                                                   w.lo[n][:, k, m * P:(m + 1) * P], cols.hi[:, k, c * CHUNK:(c + 1) * CHUNK],
                                                   cols.lo[:, k, c * CHUNK:(c + 1) * CHUNK], k == 0, k == KD - 1)
                            mm.then_inc(s_p, 1)

                    def lengths(i):
                        n, c = tasks[i]
                        pe.wait_ge(s_sqsum, i + 1)
                        if i >= 1:
                            pe.wait_ge(s_lenc, i)
                        if n == "q":
                            mm = pe.matmul(misc[:], pr.ones[:], square[:, 0, :], start=True, stop=True)
                        else:
                            for t in range(TPC):
                                mm = pe.matmul(misc[:, t:t + 1], square[:, 0, t * P:(t + 1) * P], pr.ones[:, 0:1],
                                               start=True, stop=True)
                        mm.then_inc(s_len, 1)

                    cols.turn(pe, 0)
                    cols.turn(pe, 1)
                    for i in range(len(tasks)):
                        if i + 2 < len(tasks):
                            cols.turn(pe, i + 2)
                        values(i)
                        project(i)
                        if i >= 1:
                            lengths(i - 1)
                    lengths(len(tasks) - 1)

                @block.scalar
                def _(act):
                    cols.high(act, 0, 0)
                    cols.high(act, 1, 1)
                    for i, (n, c) in enumerate(tasks):
                        if i + 2 < len(tasks):
                            cols.high(act, i + 2, i + 2)
                        act.wait_ge(s_v, i + 1)
                        act.activation(vhi[:, 2 * i:2 * i + 2, :], vbank.rearrange("p (t d) -> p t d", t=2),
                                       ACT.Copy).then_inc(s_vhi, 1)
                        for m in range(KD):
                            j = KD * i + m
                            act.wait_ge(s_p, j + 1)
                            if i >= 2:
                                act.wait_ge(s_plo, j - 3)
                            bias = pr.bias_b[:, 0 if n == "q" else 1, m:m + 1]
                            act.activation(qk32[:, i % 2, m, :], outs[:, j % 4, :], ACT.Identity, bias=bias).then_inc(s_p32, 1)
                            if i >= 1:
                                act.wait_ge(s_len, i)
                            act.activation(square[:, m, :], outs[:, j % 4, :], ACT.Square, bias=bias).then_inc(s_sq, 1)

                @block.gpsimd
                def _(pool):
                    for i in range(len(tasks)):
                        for t in (2 * i, 2 * i + 1):
                            pool.wait_ge(cols.s_xn, t + 1)
                            xv = pr.x[:, b * TILES + t, :]
                            pool.tensor_tensor(xv, xv, pr.bvo[:], ALU.add).then_inc(s_xb, 1)
                        pool.wait_ge(s_sq, KD * (i + 1))
                        first, second = square[:, 0, :], square[:, 1, :]
                        pool.tensor_tensor(first, first, second, ALU.add).then_inc(s_sqsum, 1)

                @block.vector
                def _(dve):
                    def read_lengths(i):
                        n, c = tasks[i]
                        dve.wait_ge(s_len, i + 1)
                        if n == "q":
                            dve.tensor_copy(qsq[:, c * CHUNK:(c + 1) * CHUNK], misc[:]).then_inc(s_lenc, 1)
                        else:
                            dve.tensor_scalar(nksq[:, c * TPC:(c + 1) * TPC], misc[:, 0:TPC], -1.0, None, ALU.mult).then_inc(s_lenc, 1)

                    for u in range(2):
                        cols.norm(dve, u, b, u)
                    for u in range(2):
                        cols.low(dve, u, u)
                    cols.norm(dve, 2, b, 2)
                    for i, (n, c) in enumerate(tasks):
                        if i + 3 < len(tasks):
                            cols.norm(dve, i + 3, b, i + 3)
                        if i + 2 < len(tasks):
                            cols.low(dve, i + 2, i + 2)
                        dve.wait_ge(s_vhi, i + 1)
                        dve.tensor_tensor(vlo[:, 2 * i:2 * i + 2, :], vbank.rearrange("p (t d) -> p t d", t=2),
                                          vhi[:, 2 * i:2 * i + 2, :].bitcast(F32), ALU.subtract).then_inc(s_vlo, 1)
                        for m in range(KD):
                            j = KD * i + m
                            dve.wait_ge(s_p32, j + 1)
                            cut = slice(c * CHUNK, (c + 1) * CHUNK)
                            dve.tensor_copy(hi[n][:, m, cut], qk32[:, i % 2, m, :]).then_inc(s_phi, 1)
                            dve.wait_ge(s_phi, j + 1)
                            dve.tensor_tensor(lo[n][:, m, cut], qk32[:, i % 2, m, :], hi[n][:, m, cut].bitcast(F32),
                                              ALU.subtract).then_inc(s_plo, 1)
                        if i >= 1:
                            read_lengths(i - 1)
                    read_lengths(len(tasks) - 1)

        with ExitStack() as part:
            psb = pr.sb(part)
            R = 4
            dist = psb(f"{st}_dist", [P, R, CHUNK], F32)
            score = psb(f"{st}_score", [P, 2, CHUNK], F32)
            p32 = psb(f"{st}_p32", [P, R, CHUNK], F32)
            phi = psb(f"{st}_phi", [P, R, CHUNK], F32R)
            plo = psb(f"{st}_plo", [P, R, CHUNK], F32R)
            psum_acc = w.scratch
            rden = psb(f"{st}_rden", [P, 2, TPC], F32)
            ysb = psb(f"{st}_y", [P, KD, CHUNK], F32)
            s_qk, s_dist, s_score, s_p32, s_phi, s_plo, s_acc, s_pv, s_den, s_rden, s_y = pr.sems(
                st, "qk", "dist", "score", "prob", "probhi", "problo", "acc", "pv", "den", "rden", "y")
            add_tensor, add_vector, s_rturned, s_added = add_columns(pr, st, misc, b, rden)
            next_norm = Norm(pr, st, 1 - b)
            routing = Routing(pr, st, 1 - b, misc) if b == NB - 1 else None
            steps = [(c, kt) for c in range(CHUNKS) for kt in range(TILES)]

            def summed(n):
                return (TILES - 1) * (n // TILES) + max(n % TILES, 1)

            with nc.Block() as block:
                @block.tensor
                def _(pe):
                    def scores(n):
                        c, kt = steps[n]
                        if n >= 3:
                            pe.wait_ge(s_dist, n - 2)
                        for k in range(KD):
                            mm = split_product(pe, banks[:, n % 3, :], hi["k"][:, k, kt * P:(kt + 1) * P],
                                               lo["k"][:, k, kt * P:(kt + 1) * P], hi["q"][:, k, c * CHUNK:(c + 1) * CHUNK],
                                               lo["q"][:, k, c * CHUNK:(c + 1) * CHUNK], k == 0, k == KD - 1)
                        mm.then_inc(s_qk, 1)

                    def values(n):
                        c, kt = steps[n]
                        if kt == 0 and c >= 2:
                            pe.wait_ge(s_y, KD * (c - 1))
                        pe.wait_ge(s_phi, n + 1)
                        pe.wait_ge(s_plo, n + 1)
                        for m in range(KD):
                            mm = split_product(pe, outs[:, KD * (c % 2) + m, :], vhi[:, kt, m * P:(m + 1) * P],
                                               vlo[:, kt, m * P:(m + 1) * P], phi[:, n % R, :], plo[:, n % R, :],
                                               kt == 0, kt == TILES - 1)
                        mm.then_inc(s_pv, 1)

                    def denominator(c):
                        pe.wait_ge(s_acc, (TILES - 1) * (c + 1))
                        if c >= 1:
                            pe.wait_ge(s_added, (TPC // 2) * c)
                        for t in range(TPC):
                            mm = pe.matmul(misc[:, t:t + 1], psum_acc[:, c % 2, t * P:(t + 1) * P], pr.ones[:, 0:1],
                                           start=True, stop=True)
                        mm.then_inc(s_den, 1)

                    LAG = 3
                    for n in range(len(steps) + LAG):
                        if n < len(steps):
                            scores(n)
                        if n >= LAG:
                            values(n - LAG)
                        c, at = divmod(n, TILES)
                        if 1 <= c < CHUNKS and at == 3:
                            if routing and c == 3:
                                pe.wait_ge(routing.s_logits, 1)
                            denominator(c - 1)
                        if 1 <= c < CHUNKS and at == 7:
                            pe.wait_ge(s_rden, c)
                        if 1 <= c < CHUNKS and at in (7, 9):
                            add_tensor(pe, c - 1, (at - 7) // 2, ysb, s_y)
                        if routing and (c, at) == (2, 14):
                            pe.wait_ge(s_added, (TPC // 2) * c)
                            routing.sums(pe)
                        if routing and (c, at) == (3, 1):
                            routing.products(pe)
                    denominator(CHUNKS - 1)
                    pe.wait_ge(s_rden, CHUNKS)
                    for half in range(2):
                        add_tensor(pe, CHUNKS - 1, half, ysb, s_y)

                @block.scalar
                def _(act):
                    def second(n):
                        act.wait_ge(s_score, n + 1)
                        if n >= R:
                            act.wait_ge(s_plo, n - R + 1)
                            act.wait_ge(s_acc, summed(n - R))
                        act.activation(p32[:, n % R, :], score[:, n % 2, :], ACT.Exp).then_inc(s_p32, 1)
                    def result(c):
                        act.wait_ge(s_pv, TILES * (c + 1))
                        if c >= 1:
                            act.wait_ge(s_rturned, (TPC // 2) * c)
                        for m in range(KD):
                            act.activation(ysb[:, m, :], outs[:, KD * (c % 2) + m, :], ACT.Copy).then_inc(s_y, 1)

                    for n, (c, kt) in enumerate(steps):
                        act.wait_ge(s_dist, n + 1)
                        if n >= 2:
                            act.wait_ge(s_p32, n - 1)
                        act.activation(score[:, n % 2, :], dist[:, n % R, :], ACT.Exp, scale=-1.0,
                                       bias=nksq[:, kt:kt + 1]).then_inc(s_score, 1)
                        if n >= 1:
                            second(n - 1)
                        if c >= 1 and kt == 4:
                            result(c - 1)
                    second(len(steps) - 1)
                    result(CHUNKS - 1)

                @block.gpsimd
                def _(pool):
                    done = 0
                    for n, (c, kt) in enumerate(steps):
                        if kt == 0:
                            continue
                        pool.wait_ge(s_p32, n + 1)
                        acc = psum_acc[:, c % 2, :]
                        if kt == 1:
                            if c >= 2:
                                pool.wait_ge(s_den, c - 1)
                            pool.tensor_tensor(acc, p32[:, (n - 1) % R, :], p32[:, n % R, :], ALU.add).then_inc(s_acc, 1)
                        else:
                            pool.wait_ge(s_acc, done)
                            pool.tensor_tensor(acc, acc, p32[:, n % R, :], ALU.add).then_inc(s_acc, 1)
                        done += 1

                @block.vector
                def _(dve):
                    def halves(n):
                        dve.wait_ge(s_p32, n + 1)
                        if n >= R:
                            dve.wait_ge(s_pv, n - R + 1)
                        dve.tensor_copy(phi[:, n % R, :], p32[:, n % R, :]).then_inc(s_phi, 1)
                        dve.wait_ge(s_phi, n + 1)
                        dve.tensor_tensor(plo[:, n % R, :], p32[:, n % R, :], phi[:, n % R, :].bitcast(F32), ALU.subtract)\
                           .then_inc(s_plo, 1)

                    def denominators(c):
                        dve.wait_ge(s_den, c + 1)
                        dve.reciprocal(rden[:, c % 2, :], misc[:, 0:TPC]).then_inc(s_rden, 1)

                    for n in range(len(steps) + 2):
                        if n < len(steps):
                            c, kt = steps[n]
                            dve.wait_ge(s_qk, n + 1)
                            if n >= R:
                                dve.wait_ge(s_score, n - R + 1)
                            dve.scalar_tensor_tensor(out=dist[:, n % R, :], in0=banks[:, n % 3, :], scalar=-2.0,
                                                     in1=qsq[:, c * CHUNK:(c + 1) * CHUNK], op0=ALU.mult, op1=ALU.add)\
                               .then_inc(s_dist, 1)
                        if n >= 2:
                            halves(n - 2)
                        c, at = divmod(n, TILES)
                        if 8 <= n < 8 + TILES:
                            next_norm.stats(dve, n - 8)
                        if n == 8 + TILES:
                            next_norm.guess(dve)
                        if 9 + TILES <= n < 12 + TILES:
                            next_norm.newton(dve, n - 9 - TILES)
                        if routing and n == 12 + TILES:
                            routing.shift(dve)
                        if routing and 13 + TILES <= n < 13 + 2 * TILES:
                            routing.gather(dve, n - 13 - TILES)
                        if routing and (c, at) == (3, 0):
                            routing.mean(dve)
                        if routing and (c, at) == (3, 2):
                            routing.choose(dve)
                        if 1 <= c < CHUNKS and at == 4:
                            denominators(c - 1)
                        if 1 <= c < CHUNKS and at in (7, 9):
                            add_vector(dve, c - 1, (at - 7) // 2)
                    denominators(CHUNKS - 1)
                    for half in range(2):
                        add_vector(dve, CHUNKS - 1, half)


def hybrid_block(nc, *args):
    with ExitStack() as ctx:
        pr = Program(nc, ctx, args)
        with ExitStack() as distance_ctx:
            inputs = DistanceInputs(pr, distance_ctx)
            setup(pr)
            head_attention(pr, inputs)
            pr.end_stage()
            mixture(pr, 0, last_layer=False)
            pr.end_stage()
            w = DistanceWeights(pr, distance_ctx, inputs)
            for b in range(NB):
                distance_attention(pr, b, w)
                pr.end_stage()
        mixture(pr, 1, last_layer=True)
        pr.end_stage()


_INS = ["L0_attn_a_x", "L0_attn_b_Wq", "L0_attn_b_bq", "L0_attn_b_Wk", "L0_attn_b_bk", "L0_attn_b_Wv",
        "L0_attn_b_bv", "L0_attn_b_Wo", "L0_attn_b_bo", "L0_ffn_Wr", "L0_ffn_W1", "L0_ffn_b1", "L0_ffn_W2", "L0_ffn_b2"]


def kernel(**inputs):
    import concourse.bacc as _bacc
    from concourse.bass_utils import run_bass_kernel_spmd as _run

    nc = _bacc.Bacc("TRN2", target_bir_lowering=False, num_devices=1)
    arrays, args = {}, []
    for name in _INS:
        a = np.ascontiguousarray(inputs[name])
        arrays[f"in_{name}"] = a
        args.append(nc.dram_tensor(f"in_{name}", a.shape, mybir.dt.from_np(a.dtype), kind="ExternalInput").ap())
    args.append(nc.dram_tensor("out_0", (NB, S, D), F32, kind="ExternalOutput").ap())
    hybrid_block(nc, *args)
    r = _run(nc, [arrays], core_ids=[0])
    return r.results[0]["out_0"]
```
